# Optimizing a Trainium2 kernel written in Bass

```python
import numpy as np
import jax
import jax.numpy as jnp

def _softmax(x, axis=-1):
    return jax.nn.softmax(x, axis=axis)

def _gelu(x):
    return jax.nn.gelu(x, approximate=True)

def _silu(x):
    return jax.nn.silu(x)

def _sigmoid(x):
    return jax.nn.sigmoid(x)

def _layernorm(x, axis=-1, eps=1e-05):
    m = jnp.mean(x, axis=axis, keepdims=True)
    v = jnp.var(x, axis=axis, keepdims=True)
    return (x - m) / jnp.sqrt(v + eps)

def _scatter_add(tgt, idx, src, axis=0):
    return tgt.at[idx].add(src)

def _segment_sum(src, seg, n):
    return jax.ops.segment_sum(src, seg, n)
kernel_name = 'mk_xattn_seq_d2_seqx_r8_f89237'

def setup_inputs(seed: int=0):
    np.random.seed(seed)
    _w = jnp.asarray

    def _rec_inputs():
        import jax
        import jax.numpy as jnp
        _rk = jax.random.key(seed)
        x = -0.0003929 + 0.9999 * jax.random.normal(jax.random.fold_in(_rk, 1), (128, 64, 128), jnp.float32)
        _lenS = 64 - jax.random.randint(jax.random.fold_in(_rk, 7), (128,), 0, max(1, 64 // 4) + 1, jnp.int32)
        _lenS2 = 64 - jax.random.randint(jax.random.fold_in(_rk, 8), (128,), 0, max(1, 64 // 4) + 1, jnp.int32)
        _ctx_1024P = jax.random.normal(jax.random.fold_in(_rk, 11), (128, 16, 128), jnp.float32)
        _ctx_1024c = jax.random.dirichlet(jax.random.fold_in(_rk, 511), 0.3 * jnp.ones((16,), jnp.float32), (128, 64))
        _ctx_1024t = jnp.einsum('bsk,bkd->bsd', _ctx_1024c, _ctx_1024P)
        _ctx_1024t = _ctx_1024t * jax.lax.rsqrt(jnp.mean(jnp.square(_ctx_1024t)) + 1e-12) * 0.953939
        ctx_1024 = 2.81802e-05 + 1.00001 * (_ctx_1024t + 0.3 * jax.random.normal(jax.random.fold_in(_rk, 611), (128, 64, 128), jnp.float32))
        _validS = jnp.arange(64)[None, :] < _lenS[:, None]
        _validS2 = jnp.arange(64)[None, :] < _lenS2[:, None]
        _causal = jnp.tril(jnp.ones((64, 64), dtype=bool))
        mask_BxS2_ff1 = jnp.where(jnp.ones((128, 64), dtype=bool), 1.0, 0.0).astype(jnp.float32)
        return (x, ctx_1024, mask_BxS2_ff1)
    x, ctx_1024, mask_BxS2_ff1 = _rec_inputs()

    def _L0_xattn_setup():
        import jax, jax.numpy as jnp
        import numpy as np
        LN_EPS = 1e-05
        ATTN_EPS = 1e-06
        key = jax.random.key(seed)
        k1, k2, k3 = jax.random.split(key, 3)
        B, Nq, Nk, D = (8, 256, 256, 128)
        return {'query': jax.random.normal(k1, (B, Nq, D), dtype=jnp.float32), 'key': jax.random.normal(k2, (B, Nk, D), dtype=jnp.float32), 'value': jax.random.normal(k3, (B, Nk, D), dtype=jnp.float32), 'gamma': jnp.ones((D,), dtype=jnp.float32), 'beta': jnp.zeros((D,), dtype=jnp.float32)}
    _L0_xattn_all = _L0_xattn_setup()
    _L0_xattn_in = {k: v for k, v in _L0_xattn_all.items() if k in ('gamma', 'beta')}
    del _L0_xattn_all

    def _L1_xattn_setup():
        import jax, jax.numpy as jnp
        import numpy as np
        NUM_HEADS = 16
        EMBED_DIM = 128
        HEAD_DIM = EMBED_DIM // NUM_HEADS
        N_LAYERS = 12
        B, TQ, TK = (2, 256, 256)

        def _layer_norm(x, gamma, beta, eps=1e-05):
            mean = jnp.mean(x, axis=-1, keepdims=True)
            var = jnp.var(x, axis=-1, keepdims=True)
            return (x - mean) * jax.lax.rsqrt(var + eps) * gamma + beta
        key = jax.random.key(seed)
        ks = jax.random.split(key, 8)
        target = jax.random.normal(ks[0], (B, TQ, EMBED_DIM), dtype=jnp.float32)
        context = jax.random.normal(ks[1], (B, TK, EMBED_DIM), dtype=jnp.float32)
        pad_mask = jnp.ones((B, TK), dtype=jnp.float32)
        std = 0.02
        wq = std * jax.random.normal(ks[2], (EMBED_DIM, EMBED_DIM), dtype=jnp.float32)
        wk = std * jax.random.normal(ks[3], (EMBED_DIM, EMBED_DIM), dtype=jnp.float32)
        wv = std * jax.random.normal(ks[4], (EMBED_DIM, EMBED_DIM), dtype=jnp.float32)
        proj_std = 0.02 / np.sqrt(2.0 * N_LAYERS)
        wo = proj_std * jax.random.normal(ks[5], (EMBED_DIM, EMBED_DIM), dtype=jnp.float32)
        bo = jnp.zeros((EMBED_DIM,), dtype=jnp.float32)
        ln_gamma = jnp.ones((EMBED_DIM,), dtype=jnp.float32)
        ln_beta = jnp.zeros((EMBED_DIM,), dtype=jnp.float32)
        return {'target': target, 'context': context, 'pad_mask': pad_mask, 'wq': wq, 'wk': wk, 'wv': wv, 'wo': wo, 'bo': bo, 'ln_gamma': ln_gamma, 'ln_beta': ln_beta}
    _L1_xattn_all = _L1_xattn_setup()
    _L1_xattn_in = {k: v for k, v in _L1_xattn_all.items() if k in ('wq', 'wk', 'wv', 'wo', 'bo', 'ln_gamma', 'ln_beta')}
    del _L1_xattn_all
    return {'x': x, 'ctx_1024': ctx_1024, 'mask_BxS2_ff1': mask_BxS2_ff1, 'L0_xattn_gamma': _L0_xattn_in['gamma'], 'L0_xattn_beta': _L0_xattn_in['beta'], 'L1_xattn_wq': _L1_xattn_in['wq'], 'L1_xattn_wk': _L1_xattn_in['wk'], 'L1_xattn_wv': _L1_xattn_in['wv'], 'L1_xattn_wo': _L1_xattn_in['wo'], 'L1_xattn_bo': _L1_xattn_in['bo'], 'L1_xattn_ln_gamma': _L1_xattn_in['ln_gamma'], 'L1_xattn_ln_beta': _L1_xattn_in['ln_beta']}

def reference(x, ctx_1024, mask_BxS2_ff1, L0_xattn_gamma, L0_xattn_beta, L1_xattn_wq, L1_xattn_wk, L1_xattn_wv, L1_xattn_wo, L1_xattn_bo, L1_xattn_ln_gamma, L1_xattn_ln_beta):
    import jax
    import jax.numpy as jnp

    def _L0_xattn_ref(query, key, value, gamma, beta):
        import jax, jax.numpy as jnp
        import numpy as np
        LN_EPS = 1e-05
        ATTN_EPS = 1e-06
        Q_phi = jax.nn.elu(query)
        K_phi = jax.nn.elu(key)
        KV = jnp.einsum('bnd,bne->bde', K_phi, value)
        Z = 1.0 / (jnp.einsum('bnd,bd->bn', Q_phi, K_phi.sum(axis=1)) + ATTN_EPS)
        attn = jnp.einsum('bnd,bde->bne', Q_phi, KV) * Z[..., None]
        x = query + attn
        mean = jnp.mean(x, axis=-1, keepdims=True)
        var = jnp.mean(jnp.square(x - mean), axis=-1, keepdims=True)
        return (x - mean) * jax.lax.rsqrt(var + LN_EPS) * gamma + beta

    def _L1_xattn_ref(target, context, pad_mask, wq, wk, wv, wo, bo, ln_gamma, ln_beta):
        import jax, jax.numpy as jnp
        import numpy as np
        NUM_HEADS = 16
        EMBED_DIM = 128
        HEAD_DIM = EMBED_DIM // NUM_HEADS
        N_LAYERS = 12
        B, TQ, TK = (2, 256, 256)

        def _layer_norm(x, gamma, beta, eps=1e-05):
            mean = jnp.mean(x, axis=-1, keepdims=True)
            var = jnp.var(x, axis=-1, keepdims=True)
            return (x - mean) * jax.lax.rsqrt(var + eps) * gamma + beta
        b, tq, d = target.shape
        tk = context.shape[1]
        resid = target
        q = (target @ wq).reshape(b, tq, NUM_HEADS, HEAD_DIM)
        k = (context @ wk).reshape(b, tk, NUM_HEADS, HEAD_DIM)
        v = (context @ wv).reshape(b, tk, NUM_HEADS, HEAD_DIM)
        scores = jnp.einsum('bqhd,bkhd->bhqk', q, k) * (1.0 / np.sqrt(HEAD_DIM))
        m = pad_mask[:, None, None, :]
        scores = scores * m - (1.0 - m) * jnp.asarray(10000000000.0, scores.dtype)
        attn = jax.nn.softmax(scores, axis=-1)
        out = jnp.einsum('bhqk,bkhd->bqhd', attn, v).reshape(b, tq, d)
        out = out @ wo + bo
        return _layer_norm(out + resid, ln_gamma, ln_beta)
    x = _L0_xattn_ref(x, ctx_1024, ctx_1024, L0_xattn_gamma, L0_xattn_beta)
    x = _L1_xattn_ref(x, ctx_1024, mask_BxS2_ff1, L1_xattn_wq, L1_xattn_wk, L1_xattn_wv, L1_xattn_wo, L1_xattn_bo, L1_xattn_ln_gamma, L1_xattn_ln_beta)
    return x

_drawn_inputs = setup_inputs


def setup_inputs(seed=0):
    import zlib

    import numpy as np

    out = dict(_drawn_inputs(seed))
    spreads = {'L0_xattn_gamma': (1.0, 0.2),
     'L0_xattn_beta': (0.0, 0.1),
     'L1_xattn_bo': (0.0, 0.1),
     'L1_xattn_ln_gamma': (1.0, 0.2),
     'L1_xattn_ln_beta': (0.0, 0.1)}
    factors = {'L1_xattn_wq': 8.0, 'L1_xattn_wk': 8.0, 'L1_xattn_wv': 8.0, 'L1_xattn_wo': 8.0}
    for name, (base, spread) in spreads.items():
        noise = np.random.default_rng([zlib.crc32(name.encode()), seed]).standard_normal(out[name].shape)
        drawn = base * np.exp(spread * noise) if base else spread * noise
        out[name] = jnp.asarray(drawn.astype(out[name].dtype))
    for name, factor in factors.items():
        out[name] = (out[name] * factor).astype(out[name].dtype)
    return out
```

```python
from contextlib import ExitStack

import concourse.bass as bass
from concourse import mybir

F32 = mybir.dt.float32
BF16 = mybir.dt.bfloat16
U32 = mybir.dt.uint32
ACT = mybir.ActivationFunctionType
ALU = mybir.AluOpType
AX = mybir.AxisListType

P = 128
D = 128
S = 64
HEADS, HD = 16, 8
HP = HEADS // 2
PAIRS = 4
GT = PAIRS * 2 * S
LN_EPS, ATTN_EPS, MASKED = 1e-5, 1e-6, 1e10
Q_SLOTS = (0, 0, 1, 1, 0, 2)
K_SLOTS = (0, 1, 0, 1, 2, 0)
SLOTS = len(Q_SLOTS)
R_MASK = SLOTS * 2 * HD
R_SHIFT = R_MASK + 3
R_END = R_SHIFT + 6


def xattn_kernel(nc, x, ctx_in, mask, g0, b0, wq, wk, wv, wo2, bo, g1, b1, out):
    B = x.shape[0]
    GROUPS = B // (2 * PAIRS)
    assert GROUPS % 2 == 0 and GROUPS >= 6
    xg = x.rearrange("(g j b) s d -> g (b s) j d", j=PAIRS, b=2)
    cg = ctx_in.rearrange("(g j b) s d -> g (b s) j d", j=PAIRS, b=2)
    og = out.rearrange("(g j b) s d -> g (b s) j d", j=PAIRS, b=2)
    mg = mask.rearrange("(g a) s -> g (a s)", a=2 * PAIRS)

    with ExitStack() as ctx:
        def sb(name, shape, dt=F32):
            return ctx.enter_context(nc.sbuf_tensor(name, shape, dt))

        def sem(name):
            return ctx.enter_context(nc.semaphore(name))

        def two(name, shape, dt=F32):
            return [sb(f"{name}{i}", shape, dt) for i in range(2)]

        ident = sb("ident", [P, P])
        minus_half = sb("minus_half", [P, PAIRS])
        identb = sb("identb", [P, P], BF16)
        w_q = sb("w_q", [P, D])
        w_k = sb("w_k", [P, D])
        w_v = sb("w_v", [P, D])
        w_o = sb("w_o", [P, 2, D])
        g0_col, b0_col = sb("g0_col", [P, 1]), sb("b0_col", [P, 1])
        g0_row, b0_row, bo_row = sb("g0_row", [P, D]), sb("b0_row", [P, D]), sb("bo_row", [P, D])
        g1_row, b1_row = sb("g1_row", [P, D]), sb("b1_row", [P, D])
        head_ones = sb("head_ones", [P, 2, 2, HD])
        own_batch = sb("own_batch", [P, 2])
        ones_row = sb("ones_row", [3, HP * GT], BF16)
        m_nat = sb("m_nat", [B, S])
        c_f = sb("c_f", [B, 2, S])
        c_pc = sb("c_pc", [B, 3, S], BF16)
        x_sb = two("x_sb", [P, PAIRS, D])
        c_sb = two("c_sb", [P, PAIRS, D + 1])
        mk_sb = two("mk_sb", [P, GT])
        e_sb = sb("e_sb", [P, 2, GT])
        phi = sb("phi", [P, 2, GT])
        c_t = sb("c_t", [P, GT])
        a0_sb = sb("a0_sb", [P, PAIRS, P])
        den0 = sb("den0", [P, PAIRS])
        y_sb = sb("y_sb", [P, PAIRS, D])
        st0, mv0, rs0, ve0 = sb("st0", [P, PAIRS, 6]), sb("mv0", [P, PAIRS, 2]), sb("rs0", [P, PAIRS]), sb("ve0", [P, PAIRS])
        n_sb = sb("n_sb", [P, PAIRS, D])
        res = two("res", [P, PAIRS, D])
        x1_t = sb("x1_t", [P, GT])
        k_f, r_k, r_q = sb("k_f", [P, GT]), sb("r_k", [P, GT]), sb("r_q", [P, GT])
        k_pc, q_pc = sb("k_pc", [P, 3, GT], BF16), sb("q_pc", [P, 3, GT], BF16)
        k_st = two("k_st", [P, HP, 2 * PAIRS, 2, S], BF16)
        q_st = two("q_st", [P, HP, GT], BF16)
        v_bd = two("v_bd", [P, HP, PAIRS, 2, 2, HD])
        nmax = sb("nmax", [P, PAIRS, HEADS])
        r_m = sb("r_m", [P, PAIRS, 2, HP])
        m_pc = sb("m_pc", [P, PAIRS, 2, 3, HP], BF16)
        m_t = sb("m_t", [6 * HP, GT], BF16)
        p_t = two("p_t", [P, HP, 2 * S])
        rden = sb("rden", [P, 2, 2 * S])
        o_t = two("o_t", [P, 2, 2 * S])
        y2 = sb("y2", [P, PAIRS, D])
        st1, mv1, rs1, ve1 = sb("st1", [P, PAIRS, 6]), sb("mv1", [P, PAIRS, 2]), sb("rs1", [P, PAIRS]), sb("ve1", [P, PAIRS])
        z_sb = sb("z_sb", [P, PAIRS, D])
        o_sb = two("o_sb", [P, PAIRS, D])
        c_dram = nc.dram_tensor("mask_rows", (3, B * 2 * S), BF16, kind="Internal").ap()
        c_dram_g = c_dram.rearrange("c (g t) -> g c t", t=2 * GT)

        def bank(name):
            return ctx.enter_context(nc.psum_tensor(name, [P, 512], F32))

        f_x, f_c, f_v = bank("f_x"), bank("f_c"), bank("f_v")
        s_q = [bank("s_q0"), bank("s_q1")]
        s_k = [bank("s_k0"), bank("s_k1")]
        o_ps = bank("o_ps")

        w_in, set_pool, set_dve, set_ones, c_saved, c_parts, q_ones = (
            sem("weights_in"), sem("pool_setup"), sem("dve_setup"), sem("ones_rows_in"),
            sem("mask_rows_saved"), sem("mask_parts_ready"), sem("q_scaled"))
        inputs_in = [sem("inputs_in0"), sem("inputs_in1")]
        k_stacked = [sem("k_stacked0"), sem("k_stacked1")]
        q_stacked = [sem("q_stacked0"), sem("q_stacked1")]
        shift_in = [sem("shift_in0"), sem("shift_in1")]
        out_saved = [sem("out_saved0"), sem("out_saved1")]
        transposed = sem("transposed")
        exp_ready = sem("exp_ready")
        ctxT_ready = sem("ctxT_ready")
        phi_ready = sem("phi_ready")
        a0_done = sem("a0_done")
        a0_ready = sem("a0_ready")
        k_done = sem("k_done")
        kf_ready = sem("kf_ready")
        khi_ready, kres_ready, kmid_ready, klo_ready = sem("khi"), sem("kres"), sem("kmid"), sem("klo")
        v_done = sem("v_done")
        v_ready = sem("v_ready")
        av_done = sem("av_done")
        y_ready = sem("y_ready")
        n_ready = sem("n_ready")
        nT_done = sem("nT_done")
        x1T_ready = sem("x1T_ready")
        res_ready = sem("res_ready")
        q_done = sem("q_done")
        qhi_ready, qres_ready, qmid_ready, qlo_ready = sem("qhi"), sem("qres"), sem("qmid"), sem("qlo")
        sq_done = sem("sq_done")
        max_ready = sem("max_ready")
        mpc_ready = sem("mpc_ready")
        mT_done = sem("mT_done")
        mT_ready = sem("mT_ready")
        sk_done = sem("sk_done")
        p_ready = sem("p_ready")
        pv_done = sem("pv_done")
        o_ready = sem("o_ready")
        wo_done = sem("wo_done")
        y2_ready = sem("y2_ready")
        z_ready = sem("z_ready")
        out_ready = sem("out_ready")
        front_step = sem("front_step")
        attn_step = sem("attn_step")
        pool_step = sem("pool_step")
        pool_out_step = sem("pool_out_step")
        var0_ready, rstd0_ready = sem("var0_ready"), sem("rstd0_ready")
        var1_ready, rstd1_ready = sem("var1_ready"), sem("rstd1_ready")
        DVE_FRONT, DVE_ATTN = 8, 9

        def wait(eng, s, value):
            if not (isinstance(value, int) and value <= 0):
                eng.wait_ge(s, value)

        def slots(eng, front, attention, both=None):
            def slot(u, c):
                f = (u, c) if not (isinstance(u, int) and u == 0 and c >= GROUPS) else None
                a = (u, c - 1) if not (isinstance(u, int) and u == 0 and c == 0) else None
                if both:
                    both(f, a)
                else:
                    if a:
                        attention(*a)
                    if f:
                        front(*f)
            for t in range(3):
                slot(0, t)
            with eng.Fori(1, GROUPS // 2 - 1) as u:
                slot(u, 1)
                slot(u, 2)
            slot(0, GROUPS - 1)
            slot(0, GROUPS)

        def wait_alone(eng, s, value):
            if not isinstance(value, int):
                eng.lower_val(value)
            eng.wait_ge(set_pool, 1)
            wait(eng, s, value)

        def grp(u, c):
            return 2 * u + c

        def uses(u, c):
            return u + c // 2 + 1

        block = ctx.enter_context(nc.Block())

        @block.sync
        def _(sp):
            def load(u, c):
                g, p = grp(u, c), c % 2
                wait_alone(sp, y_ready, 4 * (g - 1))
                wait_alone(sp, av_done, 2 * (g - 1))
                wait_alone(sp, kf_ready, g - 1)
                sp.dma_start(x_sb[p][:, :, :], xg[g]).then_inc(inputs_in[p], 16)
                sp.dma_start(c_sb[p][:, :, 0:D], cg[g]).then_inc(inputs_in[p], 16)
                sp.dma_start(mk_sb[p][:, :], mg[g:g + 1, :].to_broadcast([P, GT])
                             if isinstance(g, int) else mg[bass.ds(g, 1), :].to_broadcast([P, GT])
                             ).then_inc(inputs_in[p], 16)

            sp.dma_start(m_nat[:, :], mask).then_inc(c_parts, 16)
            for t, a in ((w_q, wq), (w_k, wk), (w_v, wv), (w_o, wo2)):
                sp.dma_start(t[:], a).then_inc(w_in, 16)
            load(0, 0)
            for t, a in ((g0_row, g0), (b0_row, b0), (bo_row, bo), (g1_row, g1), (b1_row, b1)):
                sp.dma_start(t[:, :], a.rearrange("(o d) -> o d", o=1).to_broadcast([P, D])).then_inc(w_in, 16)
            for t, a in ((g0_col, g0), (b0_col, b0)):
                sp.dma_start(t[:, :], a.rearrange("(d o) -> d o", o=1)).then_inc(w_in, 16)
            sp.wait_ge(set_dve, 1)
            for c in range(3):
                rows = c_dram[c:c + 1, :].rearrange("o (b a s) -> (o b) a s", a=2, s=S)
                for h2 in range(2):
                    sp.dma_start(rows[:, h2, :], c_pc[:, c, :]).then_inc(c_saved, 16)
            sp.wait_ge(set_pool, 1)
            for p in range(2):
                for h2 in range(2):
                    r = R_SHIFT + 3 * h2
                    sp.dma_start(k_st[p][r:r + 3, :, :, h2, :].rearrange("r h b t -> r (h b) t"),
                                 ones_row[:, :].rearrange("r (h t) -> r h t", t=S)).then_inc(set_ones, 16)
            sp.wait_ge(c_saved, 16 * 6)

            def stack_k(u, c):
                g, p = grp(u, c), c % 2
                wait_alone(sp, sk_done, 8 * (g - 1))
                sp.dma_start(k_st[p][R_MASK:R_SHIFT, :, :, :, :].rearrange("r h b a t -> r h (b a t)"),
                             c_dram_g[g].rearrange("c (o t) -> c o t", o=1).to_broadcast([3, HP, 2 * GT])
                             ).then_inc(k_stacked[p], 16)
                for piece, ready in ((0, khi_ready), (1, kmid_ready), (2, klo_ready)):
                    wait_alone(sp, ready, g + 1)
                    for s in range(SLOTS):
                        if K_SLOTS[s] == piece:
                            for h2 in range(2):
                                r = 16 * s + HD * h2
                                sp.dma_start(k_st[p][r:r + HD, :, :, h2, :].rearrange("r h b t -> r (h b) t"),
                                             k_pc[64 * h2:64 * h2 + 64, piece, :]).then_inc(k_stacked[p], 16)

            def stack_q(u, c):
                g, p = grp(u, c), c % 2
                for piece, ready in ((0, qhi_ready), (1, qmid_ready), (2, qlo_ready)):
                    wait_alone(sp, ready, g + 1)
                    for s in range(SLOTS):
                        if Q_SLOTS[s] == piece:
                            sp.dma_start(q_st[p][16 * s:16 * s + 16, :, :],
                                         q_pc[:, piece, :]).then_inc(q_stacked[p], 16)

            def store(u, c):
                g, p = grp(u, c), c % 2
                wait_alone(sp, out_ready, g + 1)
                sp.dma_start(og[g], o_sb[p][:, :, :]).then_inc(out_saved[p], 16)

            def both(f, a):
                if f:
                    u, c = f
                    if not (isinstance(u, int) and u == 0 and c + 1 >= GROUPS):
                        load(u, c + 1)
                    stack_k(u, c)
                    stack_q(u, c)
                if a:
                    store(*a)

            slots(sp, None, None, both)
            for p in range(2):
                sp.wait_ge(out_saved[p], 16 * (GROUPS // 2))

        @block.tensor
        def _(pe):
            mm = nc.tensor.matmul
            pe.wait_ge(w_in, 16 * 11)
            pe.wait_ge(set_pool, 1)
            pe.wait_ge(set_dve, 2)
            pe.wait_ge(q_ones, 1)
            pe.wait_ge(set_ones, 64)

            def transposes(u, c):
                g, p = grp(u, c), c % 2
                pe.wait_ge(inputs_in[p], 48 * uses(u, c))
                wait(pe, y_ready, 4 * g)
                for j in range(PAIRS):
                    last = nc.tensor.transpose(f_x[:, j * P:(j + 1) * P], x_sb[p][:, j, :], ident[:, :])
                last.then_inc(transposed, 1)
                wait(pe, qres_ready, g)
                for j in range(PAIRS):
                    last = nc.tensor.transpose(f_c[:, j * P:(j + 1) * P], c_sb[p][:, j, 0:D], ident[:, :])
                last.then_inc(transposed, 1)

            def a0_and_k(u, c):
                g = grp(u, c)
                wait(pe, phi_ready, 2 * (g + 1))
                for j in range(PAIRS):
                    t = slice(j * P, (j + 1) * P)
                    last = mm(f_x[:, t], phi[:, 1, t], phi[:, 0, t], start=True, stop=True)
                last.then_inc(a0_done, 1)
                wait(pe, ctxT_ready, g + 1)
                mm(f_c[:, :], w_k[:, :], c_t[:, :], start=True, stop=True).then_inc(k_done, 1)

            def values(u, c):
                g = grp(u, c)
                wait(pe, x1T_ready, g)
                for n in range(2 * PAIRS):
                    for h2 in range(2):
                        last = mm(f_v[S * h2:S * (h2 + 1), n * HP * HD:(n + 1) * HP * HD], c_t[:, n * S:(n + 1) * S],
                                  w_v[:, h2 * HP * HD:(h2 + 1) * HP * HD], start=True, stop=True)
                last.then_inc(v_done, 1)

            def numerators(u, c, i):
                g, p = grp(u, c), c % 2
                wait(pe, a0_ready, g + 1)
                if i == 0:
                    wait(pe, kf_ready, g + 1)
                f = (f_c, f_x)[i]
                for n in range(2):
                    j = 2 * i + n
                    last = mm(f[:, n * (D + 1):(n + 1) * (D + 1)], a0_sb[:, j, :], c_sb[p][:, j, :],
                              start=True, stop=True)
                last.then_inc(av_done, 1)

            def norm_t(u, c):
                g = grp(u, c)
                wait(pe, n_ready, g + 1)
                wait(pe, v_ready, g + 1)
                for j in range(PAIRS):
                    last = nc.tensor.transpose(f_v[:, j * P:(j + 1) * P], n_sb[:, j, :], ident[:, :])
                last.then_inc(nT_done, 1)

            def query(u, c):
                g = grp(u, c)
                wait(pe, x1T_ready, g + 1)
                wait(pe, y_ready, 4 * g + 2)
                mm(f_c[:, :], w_q[:, :], x1_t[:, :], start=True, stop=True).then_inc(q_done, 1)

            def scores_q(u, c, j):
                g, p = grp(u, c), c % 2
                if j == 0:
                    pe.wait_ge(k_stacked[p], 16 * 13 * uses(u, c))
                    pe.wait_ge(q_stacked[p], 16 * 6 * uses(u, c))
                for half in range(2):
                    if j == 0:
                        wait(pe, y2_ready, 4 * g - 1 + half)
                    else:
                        wait(pe, max_ready, 8 * g + 2 * (j - 1) + half + 1)
                    for i in range(HP // 2):
                        hp = half * (HP // 2) + i
                        for b in range(2):
                            t = slice((2 * j + b) * S, (2 * j + b + 1) * S)
                            last = mm(s_q[half][S * b:S * (b + 1), i * P:(i + 1) * P],
                                      q_st[p][0:R_SHIFT, hp, t], k_st[p][0:R_SHIFT, hp, 2 * j + b, :, :].rearrange("r a s -> r (a s)"),
                                      start=True, stop=True)
                    last.then_inc(sq_done, 1)

            def max_t(u, c):
                g = grp(u, c)
                wait_alone(pe, o_ready, 4 * g)
                wait_alone(pe, mpc_ready, g + 1)
                ob = o_ps[:, :].bitcast(BF16)
                for j in range(PAIRS):
                    last = nc.tensor.transpose(ob[0:6 * HP, j * P:(j + 1) * P],
                                               m_pc[:, j, :, :, :].rearrange("p a c h -> p (a c h)"), identb[:, :])
                last.then_inc(mT_done, 1)

            def scores_k(u, c, j, half):
                g, p = grp(u, c), c % 2
                if j == 0:
                    pe.wait_ge(shift_in[p], 16 * uses(u, c))
                    wait(pe, p_ready, 8 * (g - 1) + 6 + half + 1)
                else:
                    wait(pe, p_ready, 8 * g + 2 * (j - 1) + half + 1)
                for i in range(HP // 2):
                    hp = half * (HP // 2) + i
                    for b in range(2):
                        t = slice((2 * j + b) * S, (2 * j + b + 1) * S)
                        last = mm(s_k[half][:, i * P + S * b:i * P + S * (b + 1)],
                                  k_st[p][0:R_END, hp, 2 * j + b, :, :].rearrange("r a s -> r (a s)"), q_st[p][0:R_END, hp, t], start=True, stop=True)
                last.then_inc(sk_done, 1)

            def weigh(u, c, j, half):
                g, p = grp(u, c), c % 2
                if half == 0:
                    if j == 0:
                        wait(pe, mT_ready, g + 1)
                        wait(pe, v_ready, g + 1)
                    else:
                        wait(pe, o_ready, 4 * g + j)
                wait(pe, p_ready, 8 * g + 2 * j + half + 1)
                for i in range(HP // 2):
                    hp = half * (HP // 2) + i
                    mm(o_ps[32 * i:32 * i + 32, half * P:(half + 1) * P],
                       v_bd[p][:, hp, j, :, :, :].rearrange("p b a d -> p (b a d)"), p_t[j % 2][:, hp, :],
                       start=True, stop=True)

            def denominators(u, c, j):
                pv = p_t[j % 2][:, :, :].rearrange("p (a i) t -> p i a t", a=2)
                for i in range(HP // 2):
                    last = mm(o_ps[32 * i:32 * i + 32, 2 * P:4 * P],
                              head_ones[:, :, :, :].rearrange("p b a d -> p (b a d)"), pv[:, i, :, :],
                              start=True, stop=True)
                last.then_inc(pv_done, 1)

            def project(u, c, j):
                g = grp(u, c)
                wait(pe, o_ready, 4 * g + j + 1)
                if j < 2:
                    wait(pe, max_ready, 8 * (g + 1))
                else:
                    wait(pe, y2_ready, 4 * g + j - 1)
                for half in range(2):
                    last = mm(s_q[j % 2][:, 0:D], o_t[j % 2][:, half, :], w_o[:, half, :],
                              start=(half == 0), stop=(half == 1))
                last.then_inc(wo_done, 1)

            def both(f, a):
                if f:
                    transposes(*f)
                if a:
                    for j in range(PAIRS):
                        scores_q(*a, j)
                if f:
                    a0_and_k(*f)
                    values(*f)
                if a:
                    max_t(*a)
                if f:
                    numerators(*f, 0)
                    numerators(*f, 1)
                if a:
                    scores_k(*a, 0, 0)
                    scores_k(*a, 0, 1)
                for j in range(PAIRS):
                    if a:
                        for half in range(2):
                            weigh(*a, j, half)
                            if j + 1 < PAIRS:
                                scores_k(*a, j + 1, half)
                        denominators(*a, j)
                        if j:
                            project(*a, j - 1)
                    if f and j == 0:
                        norm_t(*f)
                    if f and j == 1:
                        query(*f)
                if a:
                    project(*a, PAIRS - 1)

            slots(pe, None, None, both)

        @block.scalar
        def _(act):
            act.wait_ge(w_in, 16 * 11)
            nc.scalar.mul(w_q[:, :], w_q[:, :], float(HD) ** -0.5).then_inc(q_ones, 1)

            def features(u, c):
                g = grp(u, c)
                wait(act, phi_ready, 2 * g)
                for i, f in enumerate((f_x, f_c)):
                    act.wait_ge(transposed, 2 * g + i + 1)
                    nc.scalar.activation(e_sb[:, i, :], f[:, :], ACT.Exp).then_inc(exp_ready, 1)
                wait(act, v_done, g)
                nc.scalar.copy(c_t[:, :], f_c[:, :]).then_inc(ctxT_ready, 1)

            def a0_copy(u, c):
                g = grp(u, c)
                wait(act, av_done, 2 * g)
                act.wait_ge(a0_done, g + 1)
                for b in range(2):
                    r = slice(S * b, S * (b + 1))
                    last = nc.scalar.copy(a0_sb[r, :, r], f_x[:, :].rearrange("p (j t) -> p j t", t=P)[r, :, r])
                last.then_inc(a0_ready, 1)

            def k_high(u, c):
                g, p = grp(u, c), c % 2
                wait(act, k_stacked[1 - p], 16 * 13 * uses(u, c - 1))
                act.wait_ge(kf_ready, g + 1)
                nc.scalar.copy(k_pc[:, 0, :], k_f[:, :]).then_inc(khi_ready, 1)

            def v_copy(u, c):
                g, p = grp(u, c), c % 2
                wait(act, pv_done, 4 * (g - 1))
                act.wait_ge(v_done, g + 1)
                v = f_v[:, :].rearrange("p (n h d) -> p h n d", n=2 * PAIRS, d=HD)
                for h2 in range(2):
                    r = slice(S * h2, S * (h2 + 1))
                    last = nc.scalar.copy(v_bd[p][r, :, :, :, h2, :].rearrange("p h j b d -> p h (j b) d"), v[r])
                last.then_inc(v_ready, 1)

            def shift(u, c):
                g, p = grp(u, c), c % 2
                wait(act, shift_in[1 - p], 16 * uses(u, c - 1))
                act.wait_ge(mT_done, g + 1)
                nc.scalar.copy(m_t[:, :], o_ps[:, :].bitcast(BF16)[0:6 * HP, 0:GT]).then_inc(mT_ready, 1)
                act.wait_ge(mT_ready, g + 1)
                act.dma_start(q_st[p][R_SHIFT:R_END, :, :], m_t[:, :]).then_inc(shift_in[p], 16)

            def exps(u, c, j):
                g = grp(u, c)
                wait(act, pv_done, 4 * g + j - 1)
                for half in range(2):
                    act.wait_ge(sk_done, 8 * g + 2 * j + half + 1)
                    n = HP // 2
                    nc.scalar.activation(p_t[j % 2][:, half * n:(half + 1) * n, :].rearrange("p h t -> p (h t)"),
                                         s_k[half][:, :], ACT.Exp).then_inc(p_ready, 1)

            def x1_transposed(u, c):
                g = grp(u, c)
                wait(act, q_done, g)
                act.wait_ge(nT_done, g + 1)
                nc.scalar.activation(x1_t[:, :], f_v[:, :], ACT.Identity, scale=g0_col[:, :],
                                     bias=b0_col[:, :]).then_inc(x1T_ready, 1)

            def q_high(u, c):
                g, p = grp(u, c), c % 2
                wait(act, q_stacked[1 - p], 16 * 6 * uses(u, c - 1))
                act.wait_ge(q_done, g + 1)
                nc.scalar.copy(q_pc[:, 0, :], f_c[:, :]).then_inc(qhi_ready, 1)

            def both(f, a):
                if f:
                    features(*f)
                    a0_copy(*f)
                    k_high(*f)
                    v_copy(*f)
                if a:
                    shift(*a)
                if a:
                    exps(*a, 0)
                    exps(*a, 1)
                if f:
                    x1_transposed(*f)
                if a:
                    exps(*a, 2)
                if f:
                    q_high(*f)
                if a:
                    exps(*a, 3)

            slots(act, None, None, both)

        @block.vector
        def _(dve):
            v = nc.vector
            v.memset(ones_row[:, :], 1.0)
            dve.wait_ge(c_parts, 16)
            v.tensor_scalar(c_f[:, 0, :], m_nat[:, :], -1.0, MASKED, ALU.add, ALU.mult).then_inc(c_parts, 1)
            dve.wait_ge(c_parts, 17)
            v.tensor_copy(c_pc[:, 0, :], c_f[:, 0, :]).then_inc(c_parts, 1)
            dve.wait_ge(c_parts, 18)
            v.tensor_tensor(c_f[:, 1, :], c_f[:, 0, :], c_pc[:, 0, :], ALU.subtract).then_inc(c_parts, 1)
            dve.wait_ge(c_parts, 19)
            v.tensor_copy(c_pc[:, 1, :], c_f[:, 1, :]).then_inc(c_parts, 1)
            dve.wait_ge(c_parts, 20)
            v.tensor_tensor(c_pc[:, 2, :], c_f[:, 1, :], c_pc[:, 1, :], ALU.subtract).then_inc(set_dve, 1)
            for p in range(2):
                v.memset(v_bd[p][:, :, :, :, :, :], 0.0)
                v.memset(c_sb[p][:, :, D:D + 1], 1.0)
                v.memset(q_st[p][R_MASK:R_SHIFT, :, :], 1.0)
            v.memset(a0_sb[:, :, :], 0.0)
            v.memset(head_ones[:, :, :, :], 0.0).then_inc(c_parts, 1)
            dve.wait_ge(c_parts, 21)
            for h2 in range(2):
                v.memset(head_ones[S * h2:S * (h2 + 1), :, h2, :], 1.0)
            dve.wait_ge(set_pool, 1)
            v.tensor_copy(identb[:, :], ident[:, :])
            v.tensor_reduce(own_batch[:, :], ident[:, :].rearrange("p (i b r) -> p b i r", b=2, r=16),
                            axis=AX.XY, op=ALU.add)
            dve.wait_ge(w_in, 16 * 11)
            v.tensor_tensor(b0_row[:, :], b0_row[:, :], bo_row[:, :], ALU.add).then_inc(set_dve, 1)
            dve.wait_ge(set_dve, 2)

            def steps(s, n, g):
                count = [0]

                def step(ins, how=wait):
                    count[0] += 1
                    ins.then_inc(s, 1)
                    how(dve, s, n * g + count[0])
                return step, count

            def features(u, c):
                g = grp(u, c)
                step, front_count = steps(front_step, DVE_FRONT, g)
                wait(dve, a0_done, g)
                for i, f in enumerate((f_x, f_c)):
                    dve.wait_ge(exp_ready, 2 * g + i + 1)
                    step(v.tensor_scalar(e_sb[:, i, :], e_sb[:, i, :], 1.0, -1.0, ALU.min, ALU.add))
                    if i == 1:
                        dve.wait_ge(ctxT_ready, g + 1)
                    v.tensor_tensor(phi[:, i, :], e_sb[:, i, :], f[:, :], ALU.max).then_inc(phi_ready, 1)
                return step, front_count

            def maxima(u, c, j):
                g = grp(u, c)
                for half in range(2):
                    dve.wait_ge(sq_done, 8 * g + 2 * j + half + 1)
                    v.tensor_reduce(nmax[:, j, half * HP:(half + 1) * HP],
                                    s_q[half][:, :].rearrange("p (h k) -> p h k", k=S),
                                    axis=AX.X, op=ALU.max, negate=True).then_inc(max_ready, 1)

            def max_pieces(u, c):
                g = grp(u, c)
                step, count = steps(attn_step, DVE_ATTN, g)
                m = nmax[:, :, :].rearrange("p j (h a) -> p j a h", a=2)
                wait(dve, mT_done, g)
                dve.wait_ge(max_ready, 8 * (g + 1))
                step(v.tensor_copy(m_pc[:, :, :, 0, :], m))
                step(v.tensor_tensor(r_m[:, :, :, :], m, m_pc[:, :, :, 0, :], ALU.subtract))
                step(v.tensor_copy(m_pc[:, :, :, 1, :], r_m[:, :, :, :]))
                v.tensor_tensor(m_pc[:, :, :, 2, :], r_m[:, :, :, :], m_pc[:, :, :, 1, :],
                                ALU.subtract).then_inc(mpc_ready, 1)
                return step, count

            def k_masked(u, c):
                g = grp(u, c)
                wait(dve, khi_ready, g)
                wait(dve, kres_ready, g)
                dve.wait_ge(k_done, g + 1)
                v.tensor_tensor(k_f[:, :], f_c[:, :], mk_sb[c % 2][:, :], ALU.mult).then_inc(kf_ready, 1)

            def k_middle(u, c):
                g, p = grp(u, c), c % 2
                wait(dve, k_stacked[1 - p], 16 * 13 * uses(u, c - 1))
                dve.wait_ge(kres_ready, g + 1)
                v.tensor_copy(k_pc[:, 1, :], r_k[:, :]).then_inc(kmid_ready, 1)

            def layer0(u, c, step):
                g, p = grp(u, c), c % 2
                for i, f in enumerate((f_c, f_x)):
                    dve.wait_ge(av_done, 2 * g + i + 1)
                    w = D + 1
                    d = den0[:, 2 * i:2 * i + 2]
                    step(v.tensor_scalar(d, f[:, 0:2 * w].rearrange("p (n w) -> p n w", w=w)[:, :, D],
                                         ATTN_EPS, None, ALU.add))
                    step(v.reciprocal(d, d))
                    for n in range(2):
                        j = 2 * i + n
                        v.scalar_tensor_tensor(out=y_sb[:, j, :], in0=f[:, n * w:n * w + D],
                                               scalar=den0[:, j:j + 1], in1=x_sb[p][:, j, :],
                                               op0=ALU.mult, op1=ALU.add).then_inc(y_ready, 1)
                for j in range(PAIRS):
                    dve.wait_ge(y_ready, 4 * g + j + 1)
                    last = v.bn_stats(st0[:, j, :], y_sb[:, j, :])
                step(last, wait_alone)
                for j in range(PAIRS):
                    last = v.bn_aggr(mv0[:, j, :], st0[:, j, :])
                step(last)
                v.tensor_scalar(ve0[:, :], mv0[:, :, 1], LN_EPS, None, ALU.add).then_inc(var0_ready, 1)
                dve.wait_ge(rstd0_ready, g + 1)
                wait(dve, nT_done, g)
                wait(dve, res_ready, g)
                for j in range(PAIRS):
                    last = v.tensor_scalar(n_sb[:, j, :], y_sb[:, j, :], mv0[:, j, 0:1], rs0[:, j:j + 1],
                                           ALU.subtract, ALU.mult)
                last.then_inc(n_ready, 1)

            def q_rest(u, c):
                g, p = grp(u, c), c % 2
                dve.wait_ge(qhi_ready, g + 1)
                wait(dve, qlo_ready, g)
                v.tensor_tensor(r_q[:, :], f_c[:, :], q_pc[:, 0, :], ALU.subtract).then_inc(qres_ready, 1)
                dve.wait_ge(qres_ready, g + 1)
                wait(dve, q_stacked[1 - p], 16 * 6 * uses(u, c - 1))
                v.tensor_copy(q_pc[:, 1, :], r_q[:, :]).then_inc(qmid_ready, 1)

            def normalise(u, c, j, step):
                g = grp(u, c)
                dve.wait_ge(pv_done, 4 * g + j + 1)
                step(v.reciprocal(rden[:, :, :].rearrange("p a t -> p (a t)"), o_ps[:, 2 * P:4 * P]))
                wait(dve, wo_done, 4 * g + j - 1)
                num = o_ps[:, 0:2 * P].rearrange("p (a t) -> p a t", a=2)
                for b in range(2):
                    t = slice(S * b, S * (b + 1))
                    last = v.scalar_tensor_tensor(out=o_t[j % 2][:, :, t], in0=num[:, :, t],
                                                  scalar=own_batch[:, b:b + 1], in1=rden[:, :, t],
                                                  op0=ALU.mult, op1=ALU.mult)
                last.then_inc(o_ready, 1)

            def residual(u, c, j):
                g, p = grp(u, c), c % 2
                if j == 0:
                    dve.wait_ge(res_ready, g + 1)
                dve.wait_ge(wo_done, 4 * g + j + 1)
                v.tensor_tensor(y2[:, j, :], s_q[j % 2][:, 0:D], res[p][:, j, :], ALU.add).then_inc(y2_ready, 1)

            def layer1_norm(u, c, step):
                g = grp(u, c)
                for j in range(PAIRS):
                    dve.wait_ge(y2_ready, 4 * g + j + 1)
                    last = v.bn_stats(st1[:, j, :], y2[:, j, :])
                step(last, wait_alone)
                for j in range(PAIRS):
                    last = v.bn_aggr(mv1[:, j, :], st1[:, j, :])
                step(last)
                v.tensor_scalar(ve1[:, :], mv1[:, :, 1], LN_EPS, None, ALU.add).then_inc(var1_ready, 1)
                dve.wait_ge(rstd1_ready, g + 1)
                wait(dve, pool_out_step, g)
                for j in range(PAIRS):
                    last = v.tensor_scalar(z_sb[:, j, :], y2[:, j, :], mv1[:, j, 0:1], rs1[:, j:j + 1],
                                           ALU.subtract, ALU.mult)
                last.then_inc(z_ready, 1)

            def both(f, a):
                if f:
                    fstep, fcount = features(*f)
                if a:
                    for j in range(PAIRS):
                        maxima(*a, j)
                    astep, acount = max_pieces(*a)
                if f:
                    k_masked(*f)
                    layer0(*f, fstep)
                    assert fcount[0] == DVE_FRONT
                    k_middle(*f)
                if a:
                    normalise(*a, 0, astep)
                    normalise(*a, 1, astep)
                    residual(*a, 0)
                if f:
                    q_rest(*f)
                if a:
                    normalise(*a, 2, astep)
                    residual(*a, 1)
                    normalise(*a, 3, astep)
                    residual(*a, 2)
                    residual(*a, 3)
                    layer1_norm(*a, astep)
                    assert acount[0] == DVE_ATTN, acount

            slots(dve, None, None, both)

        @block.gpsimd
        def _(pool):
            gp = nc.gpsimd
            gp.memset(ident[:, :], 0.0).then_inc(pool_step, 1)
            pool.wait_ge(pool_step, 1)
            gp.affine_select(out=ident[:, :], in_=ident[:, :], compare_op=ALU.not_equal, fill=1.0,
                             base=0, pattern=[[-1, P]], channel_multiplier=1)
            gp.memset(minus_half[:, :], -0.5)
            for p in range(2):
                last = gp.memset(k_st[p][:, :, :, :, :].rearrange("p h b a s -> p (h b a s)").bitcast(U32), 0)
            last.then_inc(set_pool, 1)
            pool.wait_ge(set_dve, 2)

            def k_residual(u, c):
                g = grp(u, c)
                pool.wait_ge(khi_ready, g + 1)
                gp.tensor_tensor(r_k[:, :], k_f[:, :], k_pc[:, 0, :], ALU.subtract).then_inc(kres_ready, 1)

            def k_low(u, c):
                g, p = grp(u, c), c % 2
                pool.wait_ge(kmid_ready, g + 1)
                wait(pool, k_stacked[1 - p], 16 * 13 * uses(u, c - 1))
                gp.tensor_tensor(k_pc[:, 2, :], r_k[:, :], k_pc[:, 1, :], ALU.subtract).then_inc(klo_ready, 1)

            def rstd(u, c, var_ready, ve, rs, rstd_ready):
                pool.wait_ge(var_ready, grp(u, c) + 1)
                gp.tensor_tensor(rs[:, :], ve[:, :], minus_half[:, :], ALU.pow).then_inc(rstd_ready, 1)

            def rows(row):
                return row[:, :].rearrange("p (o d) -> p o d", o=1).to_broadcast([P, PAIRS, D])

            def residual(u, c):
                g, p = grp(u, c), c % 2
                pool.wait_ge(n_ready, g + 1)
                wait(pool, y2_ready, 4 * (g - 1))
                gp.tensor_tensor(res[p][:, :, :], n_sb[:, :, :], rows(g0_row), ALU.mult).then_inc(pool_step, 1)
                pool.wait_ge(pool_step, g + 2)
                gp.tensor_tensor(res[p][:, :, :], res[p][:, :, :], rows(b0_row), ALU.add).then_inc(res_ready, 1)

            def q_low(u, c):
                g, p = grp(u, c), c % 2
                pool.wait_ge(qmid_ready, g + 1)
                wait(pool, q_stacked[1 - p], 16 * 6 * uses(u, c - 1))
                gp.tensor_tensor(q_pc[:, 2, :], r_q[:, :], q_pc[:, 1, :], ALU.subtract).then_inc(qlo_ready, 1)

            def outputs(u, c):
                g, p = grp(u, c), c % 2
                pool.wait_ge(z_ready, g + 1)
                wait(pool, out_saved[p], 16 * uses(u, c - 2))
                gp.tensor_tensor(o_sb[p][:, :, :], z_sb[:, :, :], rows(g1_row), ALU.mult).then_inc(pool_out_step, 1)
                pool.wait_ge(pool_out_step, g + 1)
                gp.tensor_tensor(o_sb[p][:, :, :], o_sb[p][:, :, :], rows(b1_row), ALU.add).then_inc(out_ready, 1)

            def both(f, a):
                if f:
                    k_residual(*f)
                    rstd(*f, var0_ready, ve0, rs0, rstd0_ready)
                    k_low(*f)
                    residual(*f)
                    q_low(*f)
                if a:
                    rstd(*a, var1_ready, ve1, rs1, rstd1_ready)
                    outputs(*a)

            slots(pool, None, None, both)


def kernel(x, ctx_1024, mask_BxS2_ff1, L0_xattn_gamma, L0_xattn_beta, L1_xattn_wq, L1_xattn_wk, L1_xattn_wv,
           L1_xattn_wo, L1_xattn_bo, L1_xattn_ln_gamma, L1_xattn_ln_beta):
    import numpy as np
    import concourse.bacc as bacc
    from concourse.bass_utils import run_bass_kernel_spmd

    def by_row(w):
        return np.asarray(w).reshape(D, HP, 2 * HD).transpose(0, 2, 1).reshape(D, D)

    wo = np.asarray(L1_xattn_wo).reshape(2, HP // 2, 1, 2 * HD, D)
    wo2 = np.repeat(wo, 2, axis=2).transpose(1, 2, 3, 0, 4).reshape(P, 2, D)
    arrays = {"x": x, "ctx": ctx_1024, "mask": mask_BxS2_ff1, "g0": L0_xattn_gamma, "b0": L0_xattn_beta,
              "wq": by_row(L1_xattn_wq), "wk": by_row(L1_xattn_wk), "wv": L1_xattn_wv, "wo2": wo2,
              "bo": L1_xattn_bo, "g1": L1_xattn_ln_gamma, "b1": L1_xattn_ln_beta}
    wv = np.asarray(L1_xattn_wv).reshape(D, HP, 2, HD).transpose(0, 2, 1, 3).reshape(D, D)
    arrays["wv"] = wv
    arrays = {f"in_{k}": np.ascontiguousarray(a) for k, a in arrays.items()}
    nc = bacc.Bacc("TRN2", target_bir_lowering=False, num_devices=1)
    args = [nc.dram_tensor(k, a.shape, F32, kind="ExternalInput").ap() for k, a in arrays.items()]
    args.append(nc.dram_tensor("out_0", x.shape, F32, kind="ExternalOutput").ap())
    xattn_kernel(nc, *args)
    r = run_bass_kernel_spmd(nc, [arrays], core_ids=[0])
    return r.results[0]["out_0"]
```

```python
from contextlib import ExitStack

import concourse.bass as bass
from concourse import mybir

F32 = mybir.dt.float32
BF16 = mybir.dt.bfloat16
U32 = mybir.dt.uint32
ACT = mybir.ActivationFunctionType
ALU = mybir.AluOpType
AX = mybir.AxisListType

P = 128
D = 128
S = 64
HEADS, HD = 16, 8
HP = HEADS // 2
PAIRS = 4
GT = PAIRS * 2 * S
LN_EPS, ATTN_EPS, MASKED = 1e-5, 1e-6, 1e10
LN_EXP_SET = 6
Q_SLOTS = (0, 0, 1, 1, 0, 2)
K_SLOTS = (0, 1, 0, 1, 2, 0)
SLOTS = len(Q_SLOTS)
R_MASK = SLOTS * 2 * HD
R_SHIFT = R_MASK + 3
R_END = R_SHIFT + 6


def xattn_kernel(nc, x, ctx_in, mask, g0, b0, wq, wk, wv, wo2, bo, g1, b1, out):
    B = x.shape[0]
    GROUPS = B // (2 * PAIRS)
    assert GROUPS % 2 == 0 and GROUPS >= 8
    xg = x.rearrange("(g j b) s d -> g (b s) j d", j=PAIRS, b=2)
    cg = ctx_in.rearrange("(g j b) s d -> g (b s) j d", j=PAIRS, b=2)
    og = out.rearrange("(g j b) s d -> g (b s) j d", j=PAIRS, b=2)
    mg = mask.rearrange("(g a) s -> g (a s)", a=2 * PAIRS)

    with ExitStack() as ctx:
        def sb(name, shape, dt=F32):
            return ctx.enter_context(nc.sbuf_tensor(name, shape, dt))

        def sem(name):
            return ctx.enter_context(nc.semaphore(name))

        def two(name, shape, dt=F32):
            return [sb(f"{name}{i}", shape, dt) for i in range(2)]

        ident = sb("ident", [P, P])
        minus_half = sb("minus_half", [P, PAIRS])
        identb = sb("identb", [P, P], BF16)
        w_q = sb("w_q", [P, D])
        w_k = sb("w_k", [P, D])
        w_v = sb("w_v", [P, D])
        w_o = sb("w_o", [P, 2, D])
        g0_col, b0_col = sb("g0_col", [P, 1]), sb("b0_col", [P, 1])
        g0_row, b0_row, bo_row = sb("g0_row", [P, D]), sb("b0_row", [P, D]), sb("bo_row", [P, D])
        g1_row, b1_row = sb("g1_row", [P, D]), sb("b1_row", [P, D])
        head_ones = sb("head_ones", [P, 2, 2, HD])
        off_batch = sb("off_batch", [P, 2])
        ones_row = sb("ones_row", [3, HP * GT], BF16)
        m_nat = sb("m_nat", [B, S])
        c_f = sb("c_f", [B, 2, S])
        c_pc = sb("c_pc", [B, 3, S], BF16)
        x_sb = two("x_sb", [P, PAIRS, D])
        c_sb = two("c_sb", [P, PAIRS, D + 1])
        mk_sb = two("mk_sb", [P, GT])
        e_sb = sb("e_sb", [P, 2, GT])
        phi = sb("phi", [P, 2, GT])
        c_t = two("c_t", [P, GT])
        a0_sb = sb("a0_sb", [P, PAIRS, P])
        den0 = sb("den0", [P, PAIRS])
        y_sb = sb("y_sb", [P, PAIRS, D])
        st0, mv0, rs0, ve0, nb0 = sb("st0", [P, PAIRS, 6]), sb("mv0", [P, PAIRS, 2]), sb("rs0", [P, PAIRS]), sb("ve0", [P, PAIRS]), sb("nb0", [P, PAIRS])
        n_sb = two("n_sb", [P, PAIRS, D])
        res = two("res", [P, PAIRS, D])
        x1_t = sb("x1_t", [P, GT])
        k_f, r_k, r_q = sb("k_f", [P, GT]), sb("r_k", [P, GT]), sb("r_q", [P, GT])
        k_pc, q_pc = sb("k_pc", [P, 3, GT], BF16), sb("q_pc", [P, 3, GT], BF16)
        k_st = two("k_st", [P, HP, 2 * PAIRS, 2, S], BF16)
        q_st = two("q_st", [P, HP, GT], BF16)
        v_bd = two("v_bd", [P, HP, PAIRS, 2, 2, HD])
        nmax = sb("nmax", [P, PAIRS, HEADS])
        r_m = sb("r_m", [P, PAIRS, 2, HP])
        m_pc = sb("m_pc", [P, PAIRS, 2, 3, HP], BF16)
        m_t = sb("m_t", [6 * HP, GT], BF16)
        p_t = two("p_t", [P, HP, 2 * S])
        lden = sb("lden", [P, 2 * 2 * S])
        rden = two("rden", [P, 2, 2 * S])
        tden = sb("tden", [P, 2, 2 * S])
        o_t = [sb(f"o_t{j}", [P, 2, 2 * S]) for j in range(PAIRS)]
        y2 = sb("y2", [P, PAIRS, D])
        st1, mv1, rs1, ve1, nb1 = sb("st1", [P, PAIRS, 6]), sb("mv1", [P, PAIRS, 2]), sb("rs1", [P, PAIRS]), sb("ve1", [P, PAIRS]), sb("nb1", [P, PAIRS])
        z_sb = sb("z_sb", [P, PAIRS, D])
        o_sb = two("o_sb", [P, PAIRS, D])
        c_dram = nc.dram_tensor("mask_rows", (3, B * 2 * S), BF16, kind="Internal").ap()
        c_dram_g = c_dram.rearrange("c (g t) -> g c t", t=2 * GT)

        def bank(name):
            return ctx.enter_context(nc.psum_tensor(name, [P, 512], F32))

        f_x, f_c, f_v = bank("f_x"), bank("f_c"), bank("f_v")
        s_k = [bank("s_k0"), bank("s_k1")]
        s_q0, s_q1, o_ps = bank("s_q0"), bank("s_q1"), bank("o_ps")
        s_q = s_k + [s_q0, s_q1]
        o_bank = (o_ps, s_q1)
        w_bank = s_q0

        w_in, set_pool, set_dve, set_ones, c_saved, c_parts, q_ones = (
            sem("weights_in"), sem("pool_setup"), sem("dve_setup"), sem("ones_rows_in"),
            sem("mask_rows_saved"), sem("mask_parts_ready"), sem("q_scaled"))
        inputs_in = [sem("inputs_in0"), sem("inputs_in1")]
        k_stacked = [sem("k_stacked0"), sem("k_stacked1")]
        q_stacked = [sem("q_stacked0"), sem("q_stacked1")]
        shift_in = [sem("shift_in0"), sem("shift_in1")]
        out_saved = [sem("out_saved0"), sem("out_saved1")]
        transposed = sem("transposed")
        exp_ready = sem("exp_ready")
        ctxT_ready = sem("ctxT_ready")
        phi_ready = sem("phi_ready")
        a0_done = sem("a0_done")
        a0_ready = sem("a0_ready")
        k_done = sem("k_done")
        kf_ready = sem("kf_ready")
        khi_ready, kres_ready, kmid_ready, klo_ready = sem("khi"), sem("kres"), sem("kmid"), sem("klo")
        v_done = sem("v_done")
        v_ready = sem("v_ready")
        av_done = sem("av_done")
        y_ready = sem("y_ready")
        n_ready = sem("n_ready")
        nT_done = sem("nT_done")
        x1T_ready = sem("x1T_ready")
        res_ready = sem("res_ready")
        q_done = sem("q_done")
        qhi_ready, qres_ready, qmid_ready, qlo_ready = sem("qhi"), sem("qres"), sem("qmid"), sem("qlo")
        sq_done = sem("sq_done")
        max_ready = sem("max_ready")
        mpc_ready = sem("mpc_ready")
        mT_done = sem("mT_done")
        mT_ready = sem("mT_ready")
        sk_done = sem("sk_done")
        p_ready = sem("p_ready")
        pv_done = sem("pv_done")
        o_ready = sem("o_ready")
        wo_done = sem("wo_done")
        y2_ready = sem("y2_ready")
        z_ready = sem("z_ready")
        out_ready = sem("out_ready")
        r0_ready = sem("r0_ready")
        ln_step = sem("ln_step")
        nb0_ready, nb1_ready = sem("nb0_ready"), sem("nb1_ready")
        pool_step = sem("pool_step")
        pool_out_step = sem("pool_out_step")
        front_step, mid_step, back_step, tail_step = (
            sem("front_step"), sem("mid_step"), sem("back_step"), sem("tail_step"))
        FRONT_STEPS, MID_STEPS, BACK_STEPS, TAIL_STEPS = 8, 3, 8, 2
        var0_ready, rstd0_ready = sem("var0_ready"), sem("rstd0_ready")
        var1_ready, rstd1_ready = sem("var1_ready"), sem("rstd1_ready")

        def wait(eng, s, value):
            if not (isinstance(value, int) and value <= 0):
                eng.wait_ge(s, value)

        NEXT, FRONT, MIDDLE, BACK, TAIL = ROLES = range(-1, 4)

        def slots(eng, slot):
            def run(u, c):
                if isinstance(u, int):
                    slot(*[(0, c - role) if 0 <= c - role < GROUPS else None for role in ROLES])
                else:
                    slot(*[(u, c - role) for role in ROLES])
            for t in range(-1, 5):
                run(0, t)
            with eng.Fori(2, GROUPS // 2 - 1) as u:
                run(u, 1)
                run(u, 2)
            for t in range(GROUPS - 1, GROUPS + 3):
                run(0, t)

        def wait_alone(eng, s, value):
            if not isinstance(value, int):
                eng.lower_val(value)
            eng.wait_ge(set_pool, 1)
            wait(eng, s, value)

        def grp(u, c):
            return 2 * u + c

        def uses(u, c):
            return u + c // 2 + 1

        block = ctx.enter_context(nc.Block())

        @block.sync
        def _(sp):
            def load(u, c):
                g, p = grp(u, c), c % 2
                wait_alone(sp, y_ready, 4 * (g - 1))
                wait_alone(sp, av_done, 2 * (g - 1))
                wait_alone(sp, kf_ready, g - 1)
                sp.dma_start(x_sb[p][:, :, :], xg[g]).then_inc(inputs_in[p], 16)
                sp.dma_start(c_sb[p][:, :, 0:D], cg[g]).then_inc(inputs_in[p], 16)
                sp.dma_start(mk_sb[p][:, :], mg[g:g + 1, :].to_broadcast([P, GT])
                             if isinstance(g, int) else mg[bass.ds(g, 1), :].to_broadcast([P, GT])
                             ).then_inc(inputs_in[p], 16)

            sp.dma_start(m_nat[:, :], mask).then_inc(c_parts, 16)
            for t, a in ((w_q, wq), (w_k, wk), (w_v, wv), (w_o, wo2)):
                sp.dma_start(t[:], a).then_inc(w_in, 16)
            load(0, 0)
            for t, a in ((g0_row, g0), (b0_row, b0), (bo_row, bo), (g1_row, g1), (b1_row, b1)):
                sp.dma_start(t[:, :], a.rearrange("(o d) -> o d", o=1).to_broadcast([P, D])).then_inc(w_in, 16)
            for t, a in ((g0_col, g0), (b0_col, b0)):
                sp.dma_start(t[:, :], a.rearrange("(d o) -> d o", o=1)).then_inc(w_in, 16)
            sp.wait_ge(set_dve, 1)
            for c in range(3):
                rows = c_dram[c:c + 1, :].rearrange("o (b a s) -> (o b) a s", a=2, s=S)
                for h2 in range(2):
                    sp.dma_start(rows[:, h2, :], c_pc[:, c, :]).then_inc(c_saved, 16)
            sp.wait_ge(set_pool, 1)
            for p in range(2):
                for h2 in range(2):
                    r = R_SHIFT + 3 * h2
                    sp.dma_start(k_st[p][r:r + 3, :, :, h2, :].rearrange("r h b t -> r (h b) t"),
                                 ones_row[:, :].rearrange("r (h t) -> r h t", t=S)).then_inc(set_ones, 16)
            sp.wait_ge(c_saved, 16 * 6)

            def stack_k(u, c):
                g, p = grp(u, c), c % 2
                wait_alone(sp, sk_done, 8 * (g - 1))
                sp.dma_start(k_st[p][R_MASK:R_SHIFT, :, :, :, :].rearrange("r h b a t -> r h (b a t)"),
                             c_dram_g[g].rearrange("c (o t) -> c o t", o=1).to_broadcast([3, HP, 2 * GT])
                             ).then_inc(k_stacked[p], 16)
                for piece, ready in ((0, khi_ready), (1, kmid_ready), (2, klo_ready)):
                    wait_alone(sp, ready, g + 1)
                    for s in range(SLOTS):
                        if K_SLOTS[s] == piece:
                            for h2 in range(2):
                                r = 16 * s + HD * h2
                                sp.dma_start(k_st[p][r:r + HD, :, :, h2, :].rearrange("r h b t -> r (h b) t"),
                                             k_pc[64 * h2:64 * h2 + 64, piece, :]).then_inc(k_stacked[p], 16)

            def stack_q(u, c):
                g, p = grp(u, c), c % 2
                wait_alone(sp, sk_done, 8 * (g - 1))
                for piece, ready in ((0, qhi_ready), (1, qmid_ready), (2, qlo_ready)):
                    wait_alone(sp, ready, g + 1)
                    for s in range(SLOTS):
                        if Q_SLOTS[s] == piece:
                            sp.dma_start(q_st[p][16 * s:16 * s + 16, :, :],
                                         q_pc[:, piece, :]).then_inc(q_stacked[p], 16)

            def store(u, c):
                g, p = grp(u, c), c % 2
                wait_alone(sp, out_ready, g + 1)
                sp.dma_start(og[g], o_sb[p][:, :, :]).then_inc(out_saved[p], 16)

            def slot(nxt, front, middle, back, tail):
                if nxt and nxt[1] > 0:
                    load(*nxt)
                if middle:
                    stack_q(*middle)
                if front:
                    stack_k(*front)
                if tail:
                    store(*tail)

            slots(sp, slot)
            for p in range(2):
                sp.wait_ge(out_saved[p], 16 * (GROUPS // 2))

        @block.tensor
        def _(pe):
            mm = nc.tensor.matmul
            pe.wait_ge(w_in, 16 * 11)
            pe.wait_ge(set_pool, 1)
            pe.wait_ge(set_dve, 2)
            pe.wait_ge(q_ones, 1)
            pe.wait_ge(set_ones, 64)

            def transposes(u, c):
                g, p = grp(u, c), c % 2
                pe.wait_ge(inputs_in[p], 48 * uses(u, c))
                wait(pe, y_ready, 4 * g)
                for j in range(PAIRS):
                    last = nc.tensor.transpose(f_x[:, j * P:(j + 1) * P], x_sb[p][:, j, :], ident[:, :])
                last.then_inc(transposed, 1)
                for j in range(PAIRS):
                    last = nc.tensor.transpose(f_c[:, j * P:(j + 1) * P], c_sb[p][:, j, 0:D], ident[:, :])
                last.then_inc(transposed, 1)

            def attention0(u, c):
                g = grp(u, c)
                wait(pe, phi_ready, 2 * (g + 1))
                for j in range(PAIRS):
                    t = slice(j * P, (j + 1) * P)
                    last = mm(f_x[:, t], phi[:, 1, t], phi[:, 0, t], start=True, stop=True)
                last.then_inc(a0_done, 1)

            def keys(u, c):
                wait(pe, ctxT_ready, grp(u, c) + 1)
                mm(f_c[:, :], w_k[:, :], c_t[c % 2][:, :], start=True, stop=True).then_inc(k_done, 1)

            def values(u, c):
                g = grp(u, c)
                wait(pe, qres_ready, g + 1)
                for n in range(2 * PAIRS):
                    for h2 in range(2):
                        last = mm(f_v[S * h2:S * (h2 + 1), n * HP * HD:(n + 1) * HP * HD], c_t[c % 2][:, n * S:(n + 1) * S],
                                  w_v[:, h2 * HP * HD:(h2 + 1) * HP * HD], start=True, stop=True)
                last.then_inc(v_done, 1)

            def numerators(u, c, i):
                g, p = grp(u, c), c % 2
                wait(pe, a0_ready, g + 1)
                if i == 0:
                    wait(pe, kf_ready, g + 1)
                f = (f_c, f_x)[i]
                for n in range(2):
                    j = 2 * i + n
                    last = mm(f[:, n * (D + 1):(n + 1) * (D + 1)], a0_sb[:, j, :], c_sb[p][:, j, :],
                              start=True, stop=True)
                last.then_inc(av_done, 1)

            def norm_t(u, c):
                g = grp(u, c)
                wait(pe, n_ready, g + 1)
                wait(pe, v_ready, g)
                for j in range(PAIRS):
                    last = nc.tensor.transpose(f_v[:, j * P:(j + 1) * P], n_sb[c % 2][:, j, :], ident[:, :])
                last.then_inc(nT_done, 1)

            def query(u, c):
                g = grp(u, c)
                wait(pe, x1T_ready, g + 1)
                mm(f_v[:, :], w_q[:, :], x1_t[:, :], start=True, stop=True).then_inc(q_done, 1)

            def scores_q(u, c, n):
                g, p = grp(u, c), c % 2
                if n == 0:
                    pe.wait_ge(k_stacked[p], 16 * 13 * uses(u, c))
                    pe.wait_ge(q_stacked[p], 16 * 6 * uses(u, c))
                if n < 2:
                    wait(pe, p_ready, 8 * g - 1 + n)
                elif n == 2:
                    wait(pe, y2_ready, 2 * g - 1)
                elif n == 3:
                    wait(pe, o_ready, 4 * g)
                else:
                    wait(pe, max_ready, 8 * g + n - 3)
                for i in range(HP // 2):
                    hp = (n % 2) * (HP // 2) + i
                    for b in range(2):
                        t = slice((n // 2 * 2 + b) * S, (n // 2 * 2 + b + 1) * S)
                        last = mm(s_q[n % 4][S * b:S * (b + 1), i * P:(i + 1) * P], q_st[p][0:R_SHIFT, hp, t],
                                  k_st[p][0:R_SHIFT, hp, n // 2 * 2 + b, :, :].rearrange("r a s -> r (a s)"),
                                  start=True, stop=True)
                last.then_inc(sq_done, 1)

            def max_t(u, c):
                g = grp(u, c)
                wait_alone(pe, o_ready, 4 * g)
                wait_alone(pe, mpc_ready, g + 1)
                ob = o_ps[:, :].bitcast(BF16)
                for j in range(PAIRS):
                    last = nc.tensor.transpose(ob[0:6 * HP, j * P:(j + 1) * P],
                                               m_pc[:, j, :, :, :].rearrange("p a c h -> p (a c h)"), identb[:, :])
                last.then_inc(mT_done, 1)

            def scores_k(u, c, j, half):
                g, p = grp(u, c), c % 2
                if j == 0:
                    pe.wait_ge(shift_in[p], 16 * uses(u, c))
                    wait(pe, max_ready, 8 * g + 5 + half)
                else:
                    wait(pe, p_ready, 8 * g + 2 * (j - 1) + half + 1)
                for i in range(HP // 2):
                    hp = half * (HP // 2) + i
                    for b in range(2):
                        t = slice((2 * j + b) * S, (2 * j + b + 1) * S)
                        last = mm(s_k[half][:, i * P + S * b:i * P + S * (b + 1)],
                                  k_st[p][0:R_END, hp, 2 * j + b, :, :].rearrange("r a s -> r (a s)"), q_st[p][0:R_END, hp, t], start=True, stop=True)
                last.then_inc(sk_done, 1)

            def weigh(u, c, j, half):
                g, p = grp(u, c), c % 2
                if half == 0:
                    if j == 0:
                        wait(pe, mT_ready, g + 1)
                        wait(pe, v_ready, g + 1)
                    elif j == 1:
                        wait(pe, max_ready, 8 * (g + 1))
                    else:
                        wait(pe, o_ready, 4 * g + j - 1)
                wait(pe, p_ready, 8 * g + 2 * j + half + 1)
                for i in range(HP // 2):
                    hp = half * (HP // 2) + i
                    mm(o_bank[j % 2][32 * i:32 * i + 32, half * P:(half + 1) * P],
                       v_bd[p][:, hp, j, :, :, :].rearrange("p b a d -> p (b a d)"), p_t[j % 2][:, hp, :],
                       start=True, stop=True)

            def denominators(u, c, j):
                pv = p_t[j % 2][:, :, :].rearrange("p (a i) t -> p i a t", a=2)
                for i in range(HP // 2):
                    last = mm(o_bank[j % 2][32 * i:32 * i + 32, 2 * P:4 * P],
                              head_ones[:, :, :, :].rearrange("p b a d -> p (b a d)"), pv[:, i, :, :],
                              start=True, stop=True)
                last.then_inc(pv_done, 1)

            def project(u, c, i, maxima_follow):
                g = grp(u, c)
                wait(pe, o_ready, 4 * g + 2 * i + 2)
                wait(pe, y2_ready, 2 * g + i)
                if i == 1 and maxima_follow:
                    wait(pe, max_ready, 8 * (g + 2))
                for n in range(2):
                    for half in range(2):
                        last = mm(w_bank[:, n * D:(n + 1) * D], o_t[2 * i + n][:, half, :], w_o[:, half, :],
                                  start=(half == 0), stop=(half == 1))
                last.then_inc(wo_done, 1)

            def slot(nxt, front, middle, back, tail):
                if back:
                    max_t(*back)
                if middle:
                    norm_t(*middle)
                if tail:
                    project(*tail, 1, back is not None)
                if middle:
                    query(*middle)
                if front:
                    attention0(*front)
                    keys(*front)
                if middle:
                    values(*middle)
                if back:
                    scores_k(*back, 0, 0)
                    scores_k(*back, 0, 1)
                if front:
                    numerators(*front, 1)
                for j in range(PAIRS):
                    if back:
                        for half in range(2):
                            weigh(*back, j, half)
                            if j + 1 < PAIRS:
                                scores_k(*back, j + 1, half)
                        denominators(*back, j)
                    if front and j == 0:
                        numerators(*front, 0)
                    if back and j == 2:
                        project(*back, 0, True)
                for n in range(2 * PAIRS):
                    if middle:
                        scores_q(*middle, n)
                    if nxt and n == 3:
                        transposes(*nxt)

            slots(pe, slot)

        @block.scalar
        def _(act):
            nc.scalar.add_instruction(mybir.InstLoadActFuncSet(
                name=nc.get_next_instruction_name(), act_func_set_id=LN_EXP_SET, ins=[], outs=[]))
            act.wait_ge(w_in, 16 * 11)
            nc.scalar.mul(w_q[:, :], w_q[:, :], float(HD) ** -0.5)
            nc.scalar.mul(w_o[:, :, :], w_o[:, :, :], -1.0).then_inc(q_ones, 1)
            act.wait_ge(set_dve, 2)

            def features(u, c):
                g = grp(u, c)
                wait(act, phi_ready, 2 * g)
                for i, f in enumerate((f_x, f_c)):
                    act.wait_ge(transposed, 2 * g + i + 1)
                    nc.scalar.activation(e_sb[:, i, :], f[:, :], ACT.Exp).then_inc(exp_ready, 1)
                wait(act, v_done, g - 1)
                nc.scalar.copy(c_t[c % 2][:, :], f_c[:, :]).then_inc(ctxT_ready, 1)

            def a0_copy(u, c):
                g = grp(u, c)
                wait(act, av_done, 2 * g)
                act.wait_ge(a0_done, g + 1)
                for b in range(2):
                    r = slice(S * b, S * (b + 1))
                    last = nc.scalar.copy(a0_sb[r, :, r], f_x[:, :].rearrange("p (j t) -> p j t", t=P)[r, :, r])
                last.then_inc(a0_ready, 1)

            def k_high(u, c):
                g, p = grp(u, c), c % 2
                wait(act, k_stacked[1 - p], 16 * 13 * uses(u, c - 1))
                act.wait_ge(kf_ready, g + 1)
                nc.scalar.copy(k_pc[:, 0, :], k_f[:, :]).then_inc(khi_ready, 1)

            def v_copy(u, c):
                g, p = grp(u, c), c % 2
                wait(act, pv_done, 4 * (g - 1))
                act.wait_ge(v_done, g + 1)
                v = f_v[:, :].rearrange("p (n h d) -> p h n d", n=2 * PAIRS, d=HD)
                for h2 in range(2):
                    r = slice(S * h2, S * (h2 + 1))
                    last = nc.scalar.copy(v_bd[p][r, :, :, :, h2, :].rearrange("p h j b d -> p h (j b) d"), v[r])
                last.then_inc(v_ready, 1)

            def shift(u, c):
                g, p = grp(u, c), c % 2
                wait(act, shift_in[1 - p], 16 * uses(u, c - 1))
                act.wait_ge(mT_done, g + 1)
                nc.scalar.copy(m_t[:, :], o_ps[:, :].bitcast(BF16)[0:6 * HP, 0:GT]).then_inc(mT_ready, 1)
                act.wait_ge(mT_ready, g + 1)
                act.dma_start(q_st[p][R_SHIFT:R_END, :, :], m_t[:, :]).then_inc(shift_in[p], 16)

            def exps(u, c, j):
                g = grp(u, c)
                wait(act, pv_done, 4 * g + j - 1)
                for half in range(2):
                    act.wait_ge(sk_done, 8 * g + 2 * j + half + 1)
                    n = HP // 2
                    nc.scalar.activation(p_t[j % 2][:, half * n:(half + 1) * n, :].rearrange("p h t -> p (h t)"),
                                         s_k[half][:, :], ACT.Exp).then_inc(p_ready, 1)

            def x1_transposed(u, c):
                g = grp(u, c)
                wait(act, q_done, g)
                act.wait_ge(nT_done, g + 1)
                nc.scalar.activation(x1_t[:, :], f_v[:, :], ACT.Identity, scale=g0_col[:, :],
                                     bias=b0_col[:, :]).then_inc(x1T_ready, 1)

            def q_high(u, c):
                g, p = grp(u, c), c % 2
                wait(act, q_stacked[1 - p], 16 * 6 * uses(u, c - 1))
                act.wait_ge(q_done, g + 1)
                nc.scalar.copy(q_pc[:, 0, :], f_v[:, :]).then_inc(qhi_ready, 1)

            def k_middle(u, c):
                act.wait_ge(kres_ready, grp(u, c) + 1)
                nc.scalar.copy(k_pc[:, 1, :], r_k[:, :]).then_inc(kmid_ready, 1)

            def q_middle(u, c):
                act.wait_ge(qres_ready, grp(u, c) + 1)
                nc.scalar.copy(q_pc[:, 1, :], r_q[:, :]).then_inc(qmid_ready, 1)

            def reciprocals(u, c, j):
                g = grp(u, c)
                act.wait_ge(pv_done, 4 * g + j + 1)
                wait(act, r0_ready, 4 * g + j)
                nc.scalar.activation(lden[:, :], o_bank[j % 2][:, 2 * P:4 * P], ACT.Ln).then_inc(ln_step, 1)
                wait(act, o_ready, 4 * g + j - 1)
                act.wait_ge(ln_step, 4 * g + j + 1)
                for b in range(2):
                    t = slice(S * b, S * (b + 1))
                    last = nc.scalar.activation(rden[j % 2][:, :, t], lden[:, :].rearrange("p (a t) -> p a t", a=2)[:, :, t],
                                                ACT.Exp, scale=-1.0, bias=off_batch[:, b:b + 1])
                last.then_inc(r0_ready, 1)

            def normalise0(u, c):
                g, p = grp(u, c), c % 2
                wait(act, res_ready, g - 1)
                act.wait_ge(nb0_ready, g + 1)
                for j in range(PAIRS):
                    last = nc.scalar.activation(n_sb[p][:, j, :], y_sb[:, j, :], ACT.Identity,
                                                scale=rs0[:, j:j + 1], bias=nb0[:, j:j + 1])
                last.then_inc(n_ready, 1)

            def normalise1(u, c):
                g = grp(u, c)
                wait(act, pool_out_step, g)
                act.wait_ge(nb1_ready, g + 1)
                for j in range(PAIRS):
                    last = nc.scalar.activation(z_sb[:, j, :], y2[:, j, :], ACT.Identity,
                                                scale=rs1[:, j:j + 1], bias=nb1[:, j:j + 1])
                last.then_inc(z_ready, 1)

            def slot(nxt, front, middle, back, tail):
                if back:
                    shift(*back)
                if middle:
                    x1_transposed(*middle)
                    q_high(*middle)
                if front:
                    a0_copy(*front)
                if middle:
                    q_middle(*middle)
                    v_copy(*middle)
                if back:
                    exps(*back, 0)
                if front:
                    k_high(*front)
                if back:
                    exps(*back, 1)
                    reciprocals(*back, 0)
                    exps(*back, 2)
                    reciprocals(*back, 1)
                if tail:
                    normalise1(*tail)
                if front:
                    k_middle(*front)
                if back:
                    exps(*back, 3)
                    reciprocals(*back, 2)
                    reciprocals(*back, 3)
                if front:
                    normalise0(*front)
                if nxt:
                    features(*nxt)

            slots(act, slot)

        @block.vector
        def _(dve):
            v = nc.vector
            v.memset(ones_row[:, :], 1.0)
            dve.wait_ge(c_parts, 16)
            v.tensor_scalar(c_f[:, 0, :], m_nat[:, :], -1.0, MASKED, ALU.add, ALU.mult).then_inc(c_parts, 1)
            dve.wait_ge(c_parts, 17)
            v.tensor_copy(c_pc[:, 0, :], c_f[:, 0, :]).then_inc(c_parts, 1)
            dve.wait_ge(c_parts, 18)
            v.tensor_tensor(c_f[:, 1, :], c_f[:, 0, :], c_pc[:, 0, :], ALU.subtract).then_inc(c_parts, 1)
            dve.wait_ge(c_parts, 19)
            v.tensor_copy(c_pc[:, 1, :], c_f[:, 1, :]).then_inc(c_parts, 1)
            dve.wait_ge(c_parts, 20)
            v.tensor_tensor(c_pc[:, 2, :], c_f[:, 1, :], c_pc[:, 1, :], ALU.subtract).then_inc(set_dve, 1)
            for p in range(2):
                v.memset(v_bd[p][:, :, :, :, :, :], 0.0)
                v.memset(c_sb[p][:, :, D:D + 1], 1.0)
                v.memset(q_st[p][R_MASK:R_SHIFT, :, :], 1.0)
            v.memset(a0_sb[:, :, :], 0.0)
            v.memset(head_ones[:, :, :, :], 0.0).then_inc(c_parts, 1)
            dve.wait_ge(c_parts, 21)
            for h2 in range(2):
                v.memset(head_ones[S * h2:S * (h2 + 1), :, h2, :], 1.0)
            dve.wait_ge(set_pool, 1)
            v.tensor_copy(identb[:, :], ident[:, :])
            v.tensor_reduce(off_batch[:, :], ident[:, :].rearrange("p (i b r) -> p b i r", b=2, r=16),
                            axis=AX.XY, op=ALU.add).then_inc(c_parts, 1)
            dve.wait_ge(c_parts, 22)
            v.tensor_scalar(off_batch[:, :], off_batch[:, :], -1.0, 1000.0, ALU.add, ALU.mult)
            dve.wait_ge(w_in, 16 * 11)
            v.tensor_tensor(b0_row[:, :], b0_row[:, :], bo_row[:, :], ALU.add).then_inc(set_dve, 1)
            dve.wait_ge(set_dve, 2)

            def steps(s, n, g):
                count = [0]

                def step(ins, how=wait):
                    count[0] += 1
                    ins.then_inc(s, 1)
                    how(dve, s, n * g + count[0])
                return step, count

            def features(u, c, step):
                g = grp(u, c)
                wait(dve, a0_done, g)
                for i, f in enumerate((f_x, f_c)):
                    dve.wait_ge(exp_ready, 2 * g + i + 1)
                    step(v.tensor_scalar(e_sb[:, i, :], e_sb[:, i, :], 1.0, -1.0, ALU.min, ALU.add))
                    if i == 1:
                        dve.wait_ge(ctxT_ready, g + 1)
                    v.tensor_tensor(phi[:, i, :], e_sb[:, i, :], f[:, :], ALU.max).then_inc(phi_ready, 1)

            def maxima(u, c, n):
                g = grp(u, c)
                dve.wait_ge(sq_done, 8 * g + n + 1)
                v.tensor_reduce(nmax[:, n // 2, (n % 2) * HP:(n % 2 + 1) * HP],
                                s_q[n % 4][:, :].rearrange("p (h k) -> p h k", k=S),
                                axis=AX.X, op=ALU.max, negate=True).then_inc(max_ready, 1)

            def max_pieces(u, c):
                g = grp(u, c)
                step, count = steps(mid_step, MID_STEPS, g)
                m = nmax[:, :, :].rearrange("p j (h a) -> p j a h", a=2)
                wait(dve, mT_done, g)
                dve.wait_ge(max_ready, 8 * (g + 1))
                step(v.tensor_copy(m_pc[:, :, :, 0, :], m))
                step(v.tensor_tensor(r_m[:, :, :, :], m, m_pc[:, :, :, 0, :], ALU.subtract))
                step(v.tensor_copy(m_pc[:, :, :, 1, :], r_m[:, :, :, :]))
                v.tensor_tensor(m_pc[:, :, :, 2, :], r_m[:, :, :, :], m_pc[:, :, :, 1, :],
                                ALU.subtract).then_inc(mpc_ready, 1)
                assert count[0] == MID_STEPS

            def k_masked(u, c):
                g = grp(u, c)
                wait(dve, khi_ready, g)
                wait(dve, kres_ready, g)
                dve.wait_ge(k_done, g + 1)
                v.tensor_tensor(k_f[:, :], f_c[:, :], mk_sb[c % 2][:, :], ALU.mult).then_inc(kf_ready, 1)

            def attended0(u, c, i, step):
                g, p = grp(u, c), c % 2
                f, w = (f_c, f_x)[i], D + 1
                dve.wait_ge(av_done, 2 * g + 2 - i)
                d = den0[:, 2 * i:2 * i + 2]
                step(v.tensor_scalar(d, f[:, 0:2 * w].rearrange("p (n w) -> p n w", w=w)[:, :, D],
                                     ATTN_EPS, None, ALU.add))
                step(v.reciprocal(d, d))
                for n in range(2):
                    j = 2 * i + n
                    v.scalar_tensor_tensor(out=y_sb[:, j, :], in0=f[:, n * w:n * w + D],
                                           scalar=den0[:, j:j + 1], in1=x_sb[p][:, j, :],
                                           op0=ALU.mult, op1=ALU.add).then_inc(y_ready, 1)

            def moments(u, c, step, y, y_done, st, mv, ve, var_ready):
                dve.wait_ge(*y_done)
                for j in range(PAIRS):
                    last = v.bn_stats(st[:, j, :], y[:, j, :])
                step(last, wait_alone)
                for j in range(PAIRS):
                    last = v.bn_aggr(mv[:, j, :], st[:, j, :])
                step(last)
                v.tensor_scalar(ve[:, :], mv[:, :, 1], LN_EPS, None, ALU.add).then_inc(var_ready, 1)

            def offset(u, c, mv, rs, nb, rstd_ready, nb_ready):
                dve.wait_ge(rstd_ready, grp(u, c) + 1)
                v.scalar_tensor_tensor(out=nb[:, :], in0=mv[:, :, 0], scalar=-1.0, in1=rs[:, :],
                                       op0=ALU.mult, op1=ALU.mult).then_inc(nb_ready, 1)

            def q_residual(u, c):
                g = grp(u, c)
                dve.wait_ge(qhi_ready, g + 1)
                wait(dve, qlo_ready, g)
                v.tensor_tensor(r_q[:, :], f_v[:, :], q_pc[:, 0, :], ALU.subtract).then_inc(qres_ready, 1)

            def normalise(u, c, j, step):
                g = grp(u, c)
                r0 = rden[j % 2][:, :, :].rearrange("p a t -> p (a t)")
                t = tden[:, :, :].rearrange("p a t -> p (a t)")
                dve.wait_ge(r0_ready, 4 * g + j + 1)
                step(v.tensor_tensor(t, o_bank[j % 2][:, 2 * P:4 * P], r0, ALU.mult))
                step(v.scalar_tensor_tensor(out=r0, in0=t, scalar=2.0, in1=r0, op0=ALU.subtract, op1=ALU.mult))
                wait(dve, wo_done, 2 * g + j // 2 - 1)
                num = o_bank[j % 2][:, 0:2 * P]
                v.tensor_tensor(o_t[j][:, :, :].rearrange("p a t -> p (a t)"), num, r0, ALU.mult).then_inc(o_ready, 1)

            def residual(u, c, i):
                g, p = grp(u, c), c % 2
                if i == 0:
                    dve.wait_ge(res_ready, g + 1)
                    wait(dve, z_ready, g)
                dve.wait_ge(wo_done, 2 * g + i + 1)
                v.tensor_tensor(y2[:, 2 * i:2 * i + 2, :],
                                w_bank[:, 0:2 * D].rearrange("p (n d) -> p n d", n=2),
                                res[p][:, 2 * i:2 * i + 2, :], ALU.add).then_inc(y2_ready, 1)

            def slot(nxt, front, middle, back, tail):
                if front:
                    fstep, fcount = steps(front_step, FRONT_STEPS, grp(*front))
                    features(*front, fstep)
                if back:
                    bstep, bcount = steps(back_step, BACK_STEPS, grp(*back))
                if tail:
                    tstep, tcount = steps(tail_step, TAIL_STEPS, grp(*tail))
                    residual(*tail, 1)
                    moments(*tail, tstep, y2, (y2_ready, 2 * grp(*tail) + 2), st1, mv1, ve1, var1_ready)
                    assert tcount[0] == TAIL_STEPS
                if middle:
                    q_residual(*middle)
                if front:
                    k_masked(*front)
                if tail:
                    offset(*tail, mv1, rs1, nb1, rstd1_ready, nb1_ready)
                if front:
                    attended0(*front, 1, fstep)
                if back:
                    normalise(*back, 0, bstep)
                if front:
                    attended0(*front, 0, fstep)
                if back:
                    normalise(*back, 1, bstep)
                if front:
                    moments(*front, fstep, y_sb, (y_ready, 4 * grp(*front) + 4), st0, mv0, ve0, var0_ready)
                    assert fcount[0] == FRONT_STEPS
                if back:
                    residual(*back, 0)
                    normalise(*back, 2, bstep)
                if front:
                    offset(*front, mv0, rs0, nb0, rstd0_ready, nb0_ready)
                if back:
                    normalise(*back, 3, bstep)
                    assert bcount[0] == BACK_STEPS
                if middle:
                    for n in range(2 * PAIRS):
                        maxima(*middle, n)
                    max_pieces(*middle)

            slots(dve, slot)

        @block.gpsimd
        def _(pool):
            gp = nc.gpsimd
            gp.memset(ident[:, :], 0.0).then_inc(pool_step, 1)
            pool.wait_ge(pool_step, 1)
            gp.affine_select(out=ident[:, :], in_=ident[:, :], compare_op=ALU.not_equal, fill=1.0,
                             base=0, pattern=[[-1, P]], channel_multiplier=1)
            gp.memset(minus_half[:, :], -0.5)
            for p in range(2):
                last = gp.memset(k_st[p][:, :, :, :, :].rearrange("p h b a s -> p (h b a s)").bitcast(U32), 0)
            last.then_inc(set_pool, 1)
            pool.wait_ge(set_dve, 2)

            def k_residual(u, c):
                g = grp(u, c)
                pool.wait_ge(khi_ready, g + 1)
                gp.tensor_tensor(r_k[:, :], k_f[:, :], k_pc[:, 0, :], ALU.subtract).then_inc(kres_ready, 1)

            def k_low(u, c):
                g, p = grp(u, c), c % 2
                pool.wait_ge(kmid_ready, g + 1)
                wait(pool, k_stacked[1 - p], 16 * 13 * uses(u, c - 1))
                gp.tensor_tensor(k_pc[:, 2, :], r_k[:, :], k_pc[:, 1, :], ALU.subtract).then_inc(klo_ready, 1)

            def rstd(u, c, var_ready, ve, rs, rstd_ready):
                pool.wait_ge(var_ready, grp(u, c) + 1)
                gp.tensor_tensor(rs[:, :], ve[:, :], minus_half[:, :], ALU.pow).then_inc(rstd_ready, 1)

            def rows(row):
                return row[:, :].rearrange("p (o d) -> p o d", o=1).to_broadcast([P, PAIRS, D])

            def residual(u, c):
                g, p = grp(u, c), c % 2
                pool.wait_ge(n_ready, g + 1)
                wait(pool, y2_ready, 2 * (g - 1))
                gp.tensor_tensor(res[p][:, :, :], n_sb[p][:, :, :], rows(g0_row), ALU.mult).then_inc(pool_step, 1)
                pool.wait_ge(pool_step, g + 2)
                gp.tensor_tensor(res[p][:, :, :], res[p][:, :, :], rows(b0_row), ALU.add).then_inc(res_ready, 1)

            def q_low(u, c):
                g, p = grp(u, c), c % 2
                pool.wait_ge(qmid_ready, g + 1)
                wait(pool, q_stacked[1 - p], 16 * 6 * uses(u, c - 1))
                gp.tensor_tensor(q_pc[:, 2, :], r_q[:, :], q_pc[:, 1, :], ALU.subtract).then_inc(qlo_ready, 1)

            def outputs(u, c):
                g, p = grp(u, c), c % 2
                pool.wait_ge(z_ready, g + 1)
                wait(pool, out_saved[p], 16 * uses(u, c - 2))
                gp.tensor_tensor(o_sb[p][:, :, :], z_sb[:, :, :], rows(g1_row), ALU.mult).then_inc(pool_out_step, 1)
                pool.wait_ge(pool_out_step, g + 1)
                gp.tensor_tensor(o_sb[p][:, :, :], o_sb[p][:, :, :], rows(b1_row), ALU.add).then_inc(out_ready, 1)

            def slot(nxt, front, middle, back, tail):
                if middle:
                    residual(*middle)
                if tail:
                    rstd(*tail, var1_ready, ve1, rs1, rstd1_ready)
                if middle:
                    q_low(*middle)
                if front:
                    k_residual(*front)
                    k_low(*front)
                    rstd(*front, var0_ready, ve0, rs0, rstd0_ready)
                if tail:
                    outputs(*tail)

            slots(pool, slot)


def kernel(x, ctx_1024, mask_BxS2_ff1, L0_xattn_gamma, L0_xattn_beta, L1_xattn_wq, L1_xattn_wk, L1_xattn_wv,
           L1_xattn_wo, L1_xattn_bo, L1_xattn_ln_gamma, L1_xattn_ln_beta):
    import numpy as np
    import concourse.bacc as bacc
    from concourse.bass_utils import run_bass_kernel_spmd

    def by_row(w):
        return np.asarray(w).reshape(D, HP, 2 * HD).transpose(0, 2, 1).reshape(D, D)

    wo = np.asarray(L1_xattn_wo).reshape(2, HP // 2, 1, 2 * HD, D)
    wo2 = np.repeat(wo, 2, axis=2).transpose(1, 2, 3, 0, 4).reshape(P, 2, D)
    arrays = {"x": x, "ctx": ctx_1024, "mask": mask_BxS2_ff1, "g0": L0_xattn_gamma, "b0": L0_xattn_beta,
              "wq": by_row(L1_xattn_wq), "wk": by_row(L1_xattn_wk), "wv": L1_xattn_wv, "wo2": wo2,
              "bo": L1_xattn_bo, "g1": L1_xattn_ln_gamma, "b1": L1_xattn_ln_beta}
    wv = np.asarray(L1_xattn_wv).reshape(D, HP, 2, HD).transpose(0, 2, 1, 3).reshape(D, D)
    arrays["wv"] = wv
    arrays = {f"in_{k}": np.ascontiguousarray(a) for k, a in arrays.items()}
    nc = bacc.Bacc("TRN2", target_bir_lowering=False, num_devices=1)
    args = [nc.dram_tensor(k, a.shape, F32, kind="ExternalInput").ap() for k, a in arrays.items()]
    args.append(nc.dram_tensor("out_0", x.shape, F32, kind="ExternalOutput").ap())
    xattn_kernel(nc, *args)
    r = run_bass_kernel_spmd(nc, [arrays], core_ids=[0])
    return r.results[0]["out_0"]
```

```python
from contextlib import ExitStack

import concourse.bass as bass
from concourse import mybir

F32 = mybir.dt.float32
BF16 = mybir.dt.bfloat16
U32 = mybir.dt.uint32
ACT = mybir.ActivationFunctionType
ALU = mybir.AluOpType
AX = mybir.AxisListType

P = 128
D = 128
S = 64
HEADS, HD = 16, 8
HP = HEADS // 2
PAIRS = 4
GT = PAIRS * 2 * S
LN_EPS, ATTN_EPS, MASKED = 1e-5, 1e-6, 1e10
LN_EXP_SET = 6
Q_SLOTS = (0, 0, 1, 1, 0, 2)
K_SLOTS = (0, 1, 0, 1, 2, 0)
SLOTS = len(Q_SLOTS)
R_MASK = SLOTS * 2 * HD
R_SHIFT = R_MASK + 3
R_END = R_SHIFT + 6


def xattn_kernel(nc, x, ctx_in, mask, g0, b0, wq, wk, wv, wo2, bo, g1, b1, out):
    B = x.shape[0]
    GROUPS = B // (2 * PAIRS)
    assert GROUPS % 2 == 0 and GROUPS >= 8
    xg = x.rearrange("(g j b) s d -> g (b s) j d", j=PAIRS, b=2)
    cg = ctx_in.rearrange("(g j b) s d -> g (b s) j d", j=PAIRS, b=2)
    og = out.rearrange("(g j b) s d -> g (b s) j d", j=PAIRS, b=2)
    mg = mask.rearrange("(g a) s -> g (a s)", a=2 * PAIRS)

    with ExitStack() as ctx:
        def sb(name, shape, dt=F32):
            return ctx.enter_context(nc.sbuf_tensor(name, shape, dt))

        def sem(name):
            return ctx.enter_context(nc.semaphore(name))

        def two(name, shape, dt=F32):
            return [sb(f"{name}{i}", shape, dt) for i in range(2)]

        ident = sb("ident", [P, P])
        minus_half = sb("minus_half", [P, PAIRS])
        ones = sb("ones", [P, PAIRS, 2, HP])
        identb = sb("identb", [P, P], BF16)
        w_q = sb("w_q", [P, D])
        w_k = sb("w_k", [P, D])
        w_v = sb("w_v", [P, D])
        w_o = sb("w_o", [P, 2, D])
        g0_col, b0_col = sb("g0_col", [P, 1]), sb("b0_col", [P, 1])
        g0_row, b0_row, bo_row = sb("g0_row", [P, D]), sb("b0_row", [P, D]), sb("bo_row", [P, D])
        g1_row, b1_row = sb("g1_row", [P, D]), sb("b1_row", [P, D])
        head_ones = sb("head_ones", [P, 2, 2, HD])
        off_batch = sb("off_batch", [P, 2])
        ones_row = sb("ones_row", [3, 1, S], BF16)
        m_nat = sb("m_nat", [B, S])
        c_f = sb("c_f", [B, 2, S])
        c_pc = sb("c_pc", [B, 3, S], BF16)
        x_sb = two("x_sb", [P, PAIRS, D])
        c_sb = two("c_sb", [P, PAIRS, D + 1])
        mk_sb = two("mk_sb", [P, GT])
        e_sb = sb("e_sb", [P, 2, GT])
        phi = sb("phi", [P, 2, GT])
        c_t = two("c_t", [P, GT])
        a0_sb = sb("a0_sb", [P, PAIRS, P])
        den0 = sb("den0", [P, PAIRS])
        y_sb = sb("y_sb", [P, PAIRS, D])
        st0, mv0 = sb("st0", [P, PAIRS, 6]), sb("mv0", [P, PAIRS, 2])
        ve0, rs0 = sb("ve0", [P, PAIRS]), sb("rs0", [P, PAIRS])
        nb0 = sb("nb0", [P, PAIRS])
        n_sb = two("n_sb", [P, PAIRS, D])
        res = two("res", [P, PAIRS, D])
        x1_t = sb("x1_t", [P, GT])
        k_f, r_k, r_q = sb("k_f", [P, GT]), sb("r_k", [P, GT]), sb("r_q", [P, GT])
        k_pc, q_pc = two("k_pc", [P, 3, GT], BF16), two("q_pc", [P, 3, GT], BF16)
        k_st = two("k_st", [P, HP, 2 * PAIRS, 2, S], BF16)
        q_st = two("q_st", [P, HP, GT], BF16)
        v_bd = two("v_bd", [P, HP, PAIRS, 2, 2, HD])
        nmax = sb("nmax", [P, PAIRS, HEADS])
        r_m = sb("r_m", [P, PAIRS, 2, HP])
        m_pc = sb("m_pc", [P, PAIRS, 2, 3, HP], BF16)
        m_t = sb("m_t", [6 * HP, GT], BF16)
        p_t = two("p_t", [P, HP, 2 * S])
        lden = sb("lden", [P, 2 * 2 * S])
        rden = two("rden", [P, 2, 2 * S])
        tden = sb("tden", [P, 2, 2 * S])
        o_t = [sb(f"o_t{j}", [P, 2, 2 * S]) for j in range(PAIRS)]
        y2 = sb("y2", [P, PAIRS, D])
        st1, mv1 = sb("st1", [P, PAIRS, 6]), sb("mv1", [P, PAIRS, 2])
        ve1, rs1 = sb("ve1", [P, PAIRS]), sb("rs1", [P, PAIRS])
        nb1 = sb("nb1", [P, PAIRS])
        z_sb = sb("z_sb", [P, PAIRS, D])
        o_sb = two("o_sb", [P, PAIRS, D])
        c_dram = nc.dram_tensor("mask_rows", (3, B * 2 * S), BF16, kind="Internal").ap()
        c_dram_g = c_dram.rearrange("c (g t) -> g c t", t=2 * GT)

        def bank(name):
            return ctx.enter_context(nc.psum_tensor(name, [P, 512], F32))

        f_x, f_c, f_v = bank("f_x"), bank("f_c"), bank("f_v")
        s_k = [bank("s_k0"), bank("s_k1")]
        w_ps = bank("w_ps")
        s_q = (f_v, w_ps)
        o_bank = (bank("o_ps0"), bank("o_ps1"))

        w_in, set_pool, set_dve, set_ones, c_saved, c_parts, k_zeroed, w_scaled = (
            sem("weights_in"), sem("pool_setup"), sem("dve_setup"), sem("ones_rows_in"),
            sem("mask_rows_saved"), sem("mask_parts_ready"), sem("stacks_zeroed"), sem("weights_scaled"))
        setup_step = sem("setup_step")
        inputs_in = [sem("inputs_in0"), sem("inputs_in1")]
        k_stacked = [sem("k_stacked0"), sem("k_stacked1")]
        q_stacked = [sem("q_stacked0"), sem("q_stacked1")]
        shift_in = [sem("shift_in0"), sem("shift_in1")]
        out_saved = [sem("out_saved0"), sem("out_saved1")]
        transposed = sem("transposed")
        exp_ready = sem("exp_ready")
        ctxT_ready = sem("ctxT_ready")
        phi_ready = sem("phi_ready")
        a0_done = sem("a0_done")
        a0_ready = sem("a0_ready")
        k_done = sem("k_done")
        kf_ready = sem("kf_ready")
        khi_ready, kres_ready, kmid_ready, klo_ready = sem("khi"), sem("kres"), sem("kmid"), sem("klo")
        v_done = sem("v_done")
        v_ready = sem("v_ready")
        av_done = sem("av_done")
        y_ready = sem("y_ready")
        n_ready = sem("n_ready")
        nT_done = sem("nT_done")
        x1T_ready = sem("x1T_ready")
        res_ready = sem("res_ready")
        q_done = sem("q_done")
        qhi_ready, qres_ready, qmid_ready, qlo_ready = sem("qhi"), sem("qres"), sem("qmid"), sem("qlo")
        sq_done = sem("sq_done")
        max_ready = sem("max_ready")
        mpc_ready = sem("mpc_ready")
        mT_done = sem("mT_done")
        mT_ready = sem("mT_ready")
        sk_done = sem("sk_done")
        p_ready = sem("p_ready")
        pv_done = sem("pv_done")
        o_ready = sem("o_ready")
        wo_done = sem("wo_done")
        y2_ready = sem("y2_ready")
        z_ready = sem("z_ready")
        out_ready = sem("out_ready")
        r0_ready = sem("r0_ready")
        ln_step = sem("ln_step")
        nb0_ready, nb1_ready = sem("nb0_ready"), sem("nb1_ready")
        pool_step = sem("pool_step")
        pool_out_step = sem("pool_out_step")
        phi_step, den0_step, stats0_step, piece_step, norm_step, stats1_step = (
            sem("phi_step"), sem("den0_step"), sem("stats0_step"), sem("piece_step"), sem("norm_step"),
            sem("stats1_step"))
        var0_ready, rstd0_ready = sem("var0_ready"), sem("rstd0_ready")
        var1_ready, rstd1_ready = sem("var1_ready"), sem("rstd1_ready")

        def wait(eng, s, value):
            if not (isinstance(value, int) and value <= 0):
                eng.wait_ge(s, value)

        LAGS = range(-1, 4)

        def slots(eng, slot):
            def run(u, c):
                if isinstance(u, int):
                    slot(*[(0, c - lag) if 0 <= c - lag < GROUPS else None for lag in LAGS])
                else:
                    slot(*[(u, c - lag) for lag in LAGS])
            for t in range(-1, 5):
                run(0, t)
            with eng.Fori(2, GROUPS // 2 - 1) as u:
                run(u, 1)
                run(u, 2)
            for t in range(GROUPS - 1, GROUPS + 3):
                run(0, t)

        def wait_alone(eng, s, value):
            if isinstance(value, int) and value <= 0:
                return
            if not isinstance(value, int):
                eng.lower_val(value)
            eng.wait_ge(set_pool, 1)
            wait(eng, s, value)

        def grp(u, c):
            return 2 * u + c

        def uses(u, c):
            return u + c // 2 + 1

        block = ctx.enter_context(nc.Block())

        @block.sync
        def _(sp):
            def load(u, c):
                g, p = grp(u, c), c % 2
                wait_alone(sp, y_ready, 4 * (g - 1))
                wait_alone(sp, av_done, 2 * (g - 1))
                wait_alone(sp, kf_ready, g - 1)
                sp.dma_start(x_sb[p][:, :, :], xg[g]).then_inc(inputs_in[p], 16)
                sp.dma_start(c_sb[p][:, :, 0:D], cg[g]).then_inc(inputs_in[p], 16)
                sp.dma_start(mk_sb[p][:, :], mg[g:g + 1, :].to_broadcast([P, GT])
                             if isinstance(g, int) else mg[bass.ds(g, 1), :].to_broadcast([P, GT])
                             ).then_inc(inputs_in[p], 16)

            load(0, 0)
            sp.dma_start(m_nat[:, :], mask).then_inc(c_parts, 16)
            for t, a in ((w_k, wk), (w_q, wq), (w_v, wv), (w_o, wo2)):
                sp.dma_start(t[:], a).then_inc(w_in, 16)
            for t, a in ((g0_row, g0), (b0_row, b0), (bo_row, bo), (g1_row, g1), (b1_row, b1)):
                sp.dma_start(t[:, :], a.rearrange("(o d) -> o d", o=1).to_broadcast([P, D])).then_inc(w_in, 16)
            for t, a in ((g0_col, g0), (b0_col, b0)):
                sp.dma_start(t[:, :], a.rearrange("(d o) -> d o", o=1)).then_inc(w_in, 16)
            sp.wait_ge(set_dve, 1)
            for a in range(2):
                sp.dma_start(c_dram.rearrange("c (b a s) -> b c a s", a=2, s=S)[:, :, a, :],
                             c_pc[:, :, :]).then_inc(c_saved, 16)
            for p in range(2):
                sp.dma_start(q_st[p][R_MASK:R_SHIFT, :, :].rearrange("r h (b t) -> r (h b) t", t=S),
                             ones_row[:, :, :].to_broadcast([3, HP * 2 * PAIRS, S])).then_inc(set_ones, 16)
            sp.wait_ge(k_zeroed, 1)
            for p in range(2):
                for h2 in range(2):
                    r = R_SHIFT + 3 * h2
                    sp.dma_start(k_st[p][r:r + 3, :, :, h2, :].rearrange("r h b t -> r (h b) t"),
                                 ones_row[:, :, :].to_broadcast([3, HP * 2 * PAIRS, S])).then_inc(set_ones, 16)
            sp.wait_ge(c_saved, 16 * 2)

            def stack_k(u, c, piece):
                g, p = grp(u, c), c % 2
                if piece == 0:
                    wait_alone(sp, sk_done, 8 * (g - 1))
                    sp.dma_start(k_st[p][R_MASK:R_SHIFT, :, :, :, :].rearrange("r h b a t -> r h (b a t)"),
                                 c_dram_g[g].rearrange("c (o t) -> c o t", o=1).to_broadcast([3, HP, 2 * GT])
                                 ).then_inc(k_stacked[p], 16)
                wait_alone(sp, (khi_ready, kmid_ready, klo_ready)[piece], g + 1)
                for s in range(SLOTS):
                    if K_SLOTS[s] == piece:
                        for h2 in range(2):
                            r = 16 * s + HD * h2
                            sp.dma_start(k_st[p][r:r + HD, :, :, h2, :].rearrange("r h b t -> r (h b) t"),
                                         k_pc[p][64 * h2:64 * h2 + 64, piece, :]).then_inc(k_stacked[p], 16)

            def stack_q(u, c, piece):
                g, p = grp(u, c), c % 2
                if piece == 0:
                    wait_alone(sp, sk_done, 8 * (g - 1))
                wait_alone(sp, (qhi_ready, qmid_ready, qlo_ready)[piece], g + 1)
                for s in range(SLOTS):
                    if Q_SLOTS[s] == piece:
                        sp.dma_start(q_st[p][16 * s:16 * s + 16, :, :],
                                     q_pc[p][:, piece, :]).then_inc(q_stacked[p], 16)

            def shift(u, c):
                g, p = grp(u, c), c % 2
                wait_alone(sp, sk_done, 8 * (g - 1))
                wait_alone(sp, mT_ready, g + 1)
                sp.dma_start(q_st[p][R_SHIFT:R_END, :, :], m_t[:, :]).then_inc(shift_in[p], 16)

            def store(u, c):
                g, p = grp(u, c), c % 2
                wait_alone(sp, out_ready, g + 1)
                sp.dma_start(og[g], o_sb[p][:, :, :]).then_inc(out_saved[p], 16)

            def slot(ahead, lag0, lag1, lag2, lag3):
                if ahead and ahead[1] > 0:
                    load(*ahead)
                if lag0:
                    stack_k(*lag0, 0)
                    stack_k(*lag0, 1)
                if lag1:
                    shift(*lag1)
                if lag0:
                    stack_k(*lag0, 2)
                    stack_q(*lag0, 0)
                    stack_q(*lag0, 1)
                    stack_q(*lag0, 2)
                if lag3:
                    store(*lag3)

            slots(sp, slot)
            for p in range(2):
                sp.wait_ge(out_saved[p], 16 * (GROUPS // 2))

        @block.tensor
        def _(pe):
            mm = nc.tensor.matmul
            pe.wait_ge(set_pool, 1)

            def transposes(u, c):
                g, p = grp(u, c), c % 2
                pe.wait_ge(inputs_in[p], 48 * uses(u, c))
                wait(pe, y_ready, 4 * g)
                for j in range(PAIRS):
                    last = nc.tensor.transpose(f_x[:, j * P:(j + 1) * P], x_sb[p][:, j, :], ident[:, :])
                last.then_inc(transposed, 1)
                for j in range(PAIRS):
                    last = nc.tensor.transpose(f_c[:, j * P:(j + 1) * P], c_sb[p][:, j, 0:D], ident[:, :])
                last.then_inc(transposed, 1)

            def attention0(u, c):
                if isinstance(u, int) and grp(u, c) == 0:
                    pe.wait_ge(set_dve, 1)
                g = grp(u, c)
                wait(pe, phi_ready, 2 * (g + 1))
                for j in range(PAIRS):
                    t = slice(j * P, (j + 1) * P)
                    last = mm(f_x[:, t], phi[:, 1, t], phi[:, 0, t], start=True, stop=True)
                last.then_inc(a0_done, 1)

            def keys(u, c):
                if isinstance(u, int) and grp(u, c) == 0:
                    pe.wait_ge(w_in, 16 * 11)
                wait(pe, phi_ready, 2 * (grp(u, c) + 1))
                wait(pe, ctxT_ready, grp(u, c) + 1)
                mm(f_c[:, :], w_k[:, :], c_t[c % 2][:, :], start=True, stop=True).then_inc(k_done, 1)

            def values(u, c):
                g = grp(u, c)
                wait(pe, qres_ready, g + 1)
                wait(pe, ctxT_ready, g + 1)
                for n in range(2 * PAIRS):
                    for h2 in range(2):
                        last = mm(f_v[S * h2:S * (h2 + 1), n * HP * HD:(n + 1) * HP * HD], c_t[c % 2][:, n * S:(n + 1) * S],
                                  w_v[:, h2 * HP * HD:(h2 + 1) * HP * HD], start=True, stop=True)
                last.then_inc(v_done, 1)

            def numerators(u, c, i):
                g, p = grp(u, c), c % 2
                wait(pe, a0_ready, g + 1)
                if i == 0:
                    wait(pe, kf_ready, g + 1)
                f = (f_c, f_x)[i]
                for n in range(2):
                    j = 2 * i + n
                    last = mm(f[:, n * (D + 1):(n + 1) * (D + 1)], a0_sb[:, j, :], c_sb[p][:, j, :],
                              start=True, stop=True)
                last.then_inc(av_done, 1)

            def norm_t(u, c):
                g = grp(u, c)
                wait(pe, n_ready, g + 1)
                wait(pe, max_ready, 8 * g - 1)
                for j in range(PAIRS):
                    last = nc.tensor.transpose(f_v[:, j * P:(j + 1) * P], n_sb[c % 2][:, j, :], ident[:, :])
                last.then_inc(nT_done, 1)

            def query(u, c):
                if isinstance(u, int) and grp(u, c) == 0:
                    pe.wait_ge(w_scaled, 1)
                g = grp(u, c)
                wait(pe, x1T_ready, g + 1)
                mm(f_v[:, :], w_q[:, :], x1_t[:, :], start=True, stop=True).then_inc(q_done, 1)

            def scores_q(u, c, n):
                if isinstance(u, int) and grp(u, c) == 0:
                    pe.wait_ge(set_ones, 16 * 6)
                g, p = grp(u, c), c % 2
                if n == 0:
                    pe.wait_ge(k_stacked[p], 16 * 13 * uses(u, c))
                    pe.wait_ge(q_stacked[p], 16 * 6 * uses(u, c))
                if n == 0:
                    wait(pe, v_ready, g + 1)
                elif n == 1:
                    wait(pe, y2_ready, g - 1)
                else:
                    wait(pe, max_ready, 8 * g + n - 1)
                for i in range(HP // 2):
                    hp = (n % 2) * (HP // 2) + i
                    for b in range(2):
                        t = slice((n // 2 * 2 + b) * S, (n // 2 * 2 + b + 1) * S)
                        last = mm(s_q[n % 2][S * b:S * (b + 1), i * P:(i + 1) * P], q_st[p][0:R_SHIFT, hp, t],
                                  k_st[p][0:R_SHIFT, hp, n // 2 * 2 + b, :, :].rearrange("r a s -> r (a s)"),
                                  start=True, stop=True)
                last.then_inc(sq_done, 1)

            def max_t(u, c):
                g = grp(u, c)
                wait_alone(pe, o_ready, 4 * g - 1)
                wait_alone(pe, mpc_ready, g + 1)
                ob = o_bank[0][:, :].bitcast(BF16)
                for j in range(PAIRS):
                    last = nc.tensor.transpose(ob[0:6 * HP, j * P:(j + 1) * P],
                                               m_pc[:, j, :, :, :].rearrange("p a c h -> p (a c h)"), identb[:, :])
                last.then_inc(mT_done, 1)

            def scores_k(u, c, j, half):
                g, p = grp(u, c), c % 2
                if j == 0:
                    pe.wait_ge(shift_in[p], 16 * uses(u, c))
                wait(pe, p_ready, 8 * g + 2 * (j - 1) + half + 1)
                for i in range(HP // 2):
                    hp = half * (HP // 2) + i
                    for b in range(2):
                        t = slice((2 * j + b) * S, (2 * j + b + 1) * S)
                        last = mm(s_k[half][:, i * P + S * b:i * P + S * (b + 1)],
                                  k_st[p][0:R_END, hp, 2 * j + b, :, :].rearrange("r a s -> r (a s)"), q_st[p][0:R_END, hp, t], start=True, stop=True)
                last.then_inc(sk_done, 1)

            def weigh(u, c, j, half):
                g, p = grp(u, c), c % 2
                if half == 0:
                    if j == 0:
                        wait(pe, mT_ready, g + 1)
                        wait(pe, v_ready, g + 1)
                    else:
                        wait(pe, o_ready, 4 * g + j - 1)
                wait(pe, p_ready, 8 * g + 2 * j + half + 1)
                for i in range(HP // 2):
                    hp = half * (HP // 2) + i
                    mm(o_bank[j % 2][32 * i:32 * i + 32, half * P:(half + 1) * P],
                       v_bd[p][:, hp, j, :, :, :].rearrange("p b a d -> p (b a d)"), p_t[j % 2][:, hp, :],
                       start=True, stop=True)

            def denominators(u, c, j):
                pv = p_t[j % 2][:, :, :].rearrange("p (a i) t -> p i a t", a=2)
                for i in range(HP // 2):
                    last = mm(o_bank[j % 2][32 * i:32 * i + 32, 2 * P:4 * P],
                              head_ones[:, :, :, :].rearrange("p b a d -> p (b a d)"), pv[:, i, :, :],
                              start=True, stop=True)
                last.then_inc(pv_done, 1)

            def project(u, c):
                g = grp(u, c)
                wait(pe, o_ready, 4 * (g + 1))
                wait(pe, y2_ready, g)
                if not (isinstance(g, int) and g == GROUPS - 1):
                    wait(pe, max_ready, 8 * (g + 2))
                for j in range(PAIRS):
                    for half in range(2):
                        last = mm(w_ps[:, j * D:(j + 1) * D], o_t[j][:, half, :], w_o[:, half, :],
                                  start=(half == 0), stop=(half == 1))
                last.then_inc(wo_done, 1)

            def slot(ahead, lag0, lag1, lag2, lag3):
                if lag3:
                    scores_k(*lag3, 0, 0)
                    scores_k(*lag3, 0, 1)
                if lag1:
                    numerators(*lag1, 0)
                if lag3:
                    weigh(*lag3, 0, 0)
                    scores_k(*lag3, 1, 0)
                    weigh(*lag3, 0, 1)
                    scores_k(*lag3, 1, 1)
                    denominators(*lag3, 0)
                if lag2:
                    values(*lag2)
                if lag3:
                    weigh(*lag3, 1, 0)
                    scores_k(*lag3, 2, 0)
                    weigh(*lag3, 1, 1)
                    denominators(*lag3, 1)
                if lag2:
                    scores_q(*lag2, 0)
                if lag3:
                    scores_k(*lag3, 2, 1)
                if lag2:
                    scores_q(*lag2, 1)
                if lag3:
                    scores_k(*lag3, 3, 0)
                    weigh(*lag3, 2, 0)
                if lag2:
                    scores_q(*lag2, 2)
                if lag3:
                    scores_k(*lag3, 3, 1)
                if lag2:
                    scores_q(*lag2, 3)
                if lag3:
                    weigh(*lag3, 2, 1)
                if lag2:
                    scores_q(*lag2, 4)
                    scores_q(*lag2, 5)
                if lag3:
                    denominators(*lag3, 2)
                if lag2:
                    scores_q(*lag2, 6)
                    scores_q(*lag2, 7)
                if lag0:
                    transposes(*lag0)
                if lag1:
                    norm_t(*lag1)
                if lag3:
                    weigh(*lag3, 3, 0)
                    weigh(*lag3, 3, 1)
                    denominators(*lag3, 3)
                if lag2:
                    max_t(*lag2)
                if lag1:
                    query(*lag1)
                if lag0:
                    attention0(*lag0)
                    keys(*lag0)
                if lag3:
                    project(*lag3)
                if lag0:
                    numerators(*lag0, 1)

            slots(pe, slot)

        @block.scalar
        def _(act):
            nc.scalar.add_instruction(mybir.InstLoadActFuncSet(
                name=nc.get_next_instruction_name(), act_func_set_id=LN_EXP_SET, ins=[], outs=[]))
            act.wait_ge(set_dve, 1)

            def features(u, c, i):
                g = grp(u, c)
                wait(act, phi_ready, 2 * g + i - 1)
                act.wait_ge(transposed, 2 * g + i + 1)
                nc.scalar.activation(e_sb[:, i, :], (f_x, f_c)[i][:, :], ACT.Exp).then_inc(exp_ready, 1)

            def ctx_transposed(u, c):
                g = grp(u, c)
                wait(act, v_done, g - 1)
                act.wait_ge(transposed, 2 * g + 2)
                nc.scalar.copy(c_t[c % 2][:, :], f_c[:, :]).then_inc(ctxT_ready, 1)

            def a0_copy(u, c):
                g = grp(u, c)
                wait(act, av_done, 2 * g)
                act.wait_ge(a0_done, g + 1)
                for b in range(2):
                    r = slice(S * b, S * (b + 1))
                    last = nc.scalar.copy(a0_sb[r, :, r], f_x[:, :].rearrange("p (j t) -> p j t", t=P)[r, :, r])
                last.then_inc(a0_ready, 1)

            def k_high(u, c):
                g, p = grp(u, c), c % 2
                wait(act, k_stacked[p], 16 * 13 * uses(u, c - 2))
                act.wait_ge(kf_ready, g + 1)
                nc.scalar.copy(k_pc[p][:, 0, :], k_f[:, :]).then_inc(khi_ready, 1)

            def v_copy(u, c):
                g, p = grp(u, c), c % 2
                wait(act, pv_done, 4 * (g - 1))
                act.wait_ge(v_done, g + 1)
                v = f_v[:, :].rearrange("p (n h d) -> p h n d", n=2 * PAIRS, d=HD)
                for h2 in range(2):
                    r = slice(S * h2, S * (h2 + 1))
                    last = nc.scalar.copy(v_bd[p][r, :, :, :, h2, :].rearrange("p h j b d -> p h (j b) d"), v[r])
                last.then_inc(v_ready, 1)

            def maxima_copy(u, c):
                g, p = grp(u, c), c % 2
                wait(act, shift_in[1 - p], 16 * uses(u, c - 1))
                act.wait_ge(mT_done, g + 1)
                nc.scalar.copy(m_t[:, :], o_bank[0][:, :].bitcast(BF16)[0:6 * HP, 0:GT]).then_inc(mT_ready, 1)

            def exps(u, c, j, half):
                g = grp(u, c)
                wait(act, pv_done, 4 * g + j - 1)
                act.wait_ge(sk_done, 8 * g + 2 * j + half + 1)
                n = HP // 2
                nc.scalar.activation(p_t[j % 2][:, half * n:(half + 1) * n, :].rearrange("p h t -> p (h t)"),
                                     s_k[half][:, :], ACT.Exp).then_inc(p_ready, 1)

            def x1_transposed(u, c):
                g = grp(u, c)
                wait(act, q_done, g)
                act.wait_ge(nT_done, g + 1)
                if isinstance(g, int) and g == 0:
                    act.wait_ge(w_in, 16 * 11)
                nc.scalar.activation(x1_t[:, :], f_v[:, :], ACT.Identity, scale=g0_col[:, :],
                                     bias=b0_col[:, :]).then_inc(x1T_ready, 1)

            def q_high(u, c):
                g, p = grp(u, c), c % 2
                wait(act, q_stacked[p], 16 * 6 * uses(u, c - 2))
                act.wait_ge(q_done, g + 1)
                nc.scalar.copy(q_pc[p][:, 0, :], f_v[:, :]).then_inc(qhi_ready, 1)

            def k_middle(u, c):
                g, p = grp(u, c), c % 2
                wait(act, k_stacked[p], 16 * 13 * uses(u, c - 2))
                act.wait_ge(kres_ready, g + 1)
                nc.scalar.copy(k_pc[p][:, 1, :], r_k[:, :]).then_inc(kmid_ready, 1)

            def q_middle(u, c):
                g, p = grp(u, c), c % 2
                wait(act, q_stacked[p], 16 * 6 * uses(u, c - 2))
                act.wait_ge(qres_ready, g + 1)
                nc.scalar.copy(q_pc[p][:, 1, :], r_q[:, :]).then_inc(qmid_ready, 1)

            def logarithms(u, c, j):
                n = 4 * grp(u, c) + j
                wait(act, r0_ready, n)
                act.wait_ge(pv_done, n + 1)
                nc.scalar.activation(lden[:, :], o_bank[j % 2][:, 2 * P:4 * P], ACT.Ln).then_inc(ln_step, 1)

            def reciprocals(u, c, j):
                n = 4 * grp(u, c) + j
                wait(act, o_ready, n - 1)
                act.wait_ge(ln_step, n + 1)
                for b in range(2):
                    t = slice(S * b, S * (b + 1))
                    last = nc.scalar.activation(rden[j % 2][:, :, t], lden[:, :].rearrange("p (a t) -> p a t", a=2)[:, :, t],
                                                ACT.Exp, scale=-1.0, bias=off_batch[:, b:b + 1])
                last.then_inc(r0_ready, 1)

            def normalise0(u, c):
                g, p = grp(u, c), c % 2
                wait(act, res_ready, g - 1)
                act.wait_ge(nb0_ready, g + 1)
                for j in range(PAIRS):
                    last = nc.scalar.activation(n_sb[p][:, j, :], y_sb[:, j, :], ACT.Identity,
                                                scale=rs0[:, j:j + 1], bias=nb0[:, j:j + 1])
                last.then_inc(n_ready, 1)

            def normalise1(u, c):
                g = grp(u, c)
                wait(act, pool_out_step, g)
                act.wait_ge(nb1_ready, g + 1)
                for j in range(PAIRS):
                    last = nc.scalar.activation(z_sb[:, j, :], y2[:, j, :], ACT.Identity,
                                                scale=rs1[:, j:j + 1], bias=nb1[:, j:j + 1])
                last.then_inc(z_ready, 1)

            def slot(ahead, lag0, lag1, lag2, lag3):
                if lag0:
                    a0_copy(*lag0)
                    k_high(*lag0)
                if lag2:
                    exps(*lag2, 0, 0)
                    exps(*lag2, 0, 1)
                    exps(*lag2, 1, 0)
                    exps(*lag2, 1, 1)
                    logarithms(*lag2, 0)
                    reciprocals(*lag2, 0)
                if lag1:
                    v_copy(*lag1)
                if lag2:
                    exps(*lag2, 2, 0)
                    logarithms(*lag2, 1)
                    reciprocals(*lag2, 1)
                    exps(*lag2, 2, 1)
                if lag0:
                    k_middle(*lag0)
                if lag2:
                    exps(*lag2, 3, 0)
                    exps(*lag2, 3, 1)
                if lag0:
                    normalise0(*lag0)
                if lag2:
                    logarithms(*lag2, 2)
                    reciprocals(*lag2, 2)
                if ahead:
                    features(*ahead, 0)
                    features(*ahead, 1)
                    ctx_transposed(*ahead)
                if lag0:
                    x1_transposed(*lag0)
                if lag2:
                    logarithms(*lag2, 3)
                if lag1:
                    maxima_copy(*lag1)
                if lag2:
                    reciprocals(*lag2, 3)
                if lag0:
                    q_high(*lag0)
                if lag3:
                    normalise1(*lag3)
                if lag0:
                    q_middle(*lag0)

            slots(act, slot)

        @block.vector
        def _(dve):
            v = nc.vector
            v.memset(ones_row[:, :, :], 1.0)
            v.memset(a0_sb[:, :, :], 0.0)
            for p in range(2):
                v.memset(c_sb[p][:, :, D:D + 1], 1.0)
            v.memset(head_ones[:, :, :, :], 0.0).then_inc(setup_step, 1)
            dve.wait_ge(setup_step, 1)
            for h2 in range(2):
                v.memset(head_ones[S * h2:S * (h2 + 1), :, h2, :], 1.0)
            dve.wait_ge(set_pool, 1)
            v.tensor_copy(identb[:, :], ident[:, :])
            v.tensor_reduce(off_batch[:, :], ident[:, :].rearrange("p (i b r) -> p b i r", b=2, r=16),
                            axis=AX.XY, op=ALU.add).then_inc(setup_step, 1)
            dve.wait_ge(setup_step, 2)
            v.tensor_scalar(off_batch[:, :], off_batch[:, :], -1.0, 1000.0, ALU.add, ALU.mult)
            for p in range(2):
                v.memset(v_bd[p][:, :, :, :, :, :], 0.0)
            dve.wait_ge(c_parts, 16)
            v.tensor_scalar(c_f[:, 0, :], m_nat[:, :], -1.0, MASKED, ALU.add, ALU.mult).then_inc(c_parts, 1)
            dve.wait_ge(c_parts, 17)
            v.tensor_copy(c_pc[:, 0, :], c_f[:, 0, :]).then_inc(c_parts, 1)
            dve.wait_ge(c_parts, 18)
            v.tensor_tensor(c_f[:, 1, :], c_f[:, 0, :], c_pc[:, 0, :], ALU.subtract).then_inc(c_parts, 1)
            dve.wait_ge(c_parts, 19)
            v.tensor_copy(c_pc[:, 1, :], c_f[:, 1, :]).then_inc(c_parts, 1)
            dve.wait_ge(c_parts, 20)
            v.tensor_tensor(c_pc[:, 2, :], c_f[:, 1, :], c_pc[:, 1, :], ALU.subtract).then_inc(set_dve, 1)

            def flat(t):
                return t[:, :, :].rearrange("p a t -> p (a t)")

            def clip(u, c, i):
                g = grp(u, c)
                dve.wait_ge(exp_ready, 2 * g + i + 1)
                v.tensor_scalar(e_sb[:, i, :], e_sb[:, i, :], 1.0, -1.0, ALU.min, ALU.add).then_inc(phi_step, 1)

            def features(u, c, i):
                g = grp(u, c)
                wait(dve, a0_done, g)
                if i == 1:
                    dve.wait_ge(ctxT_ready, g + 1)
                dve.wait_ge(phi_step, 2 * g + i + 1)
                v.tensor_tensor(phi[:, i, :], e_sb[:, i, :], (f_x, f_c)[i][:, :], ALU.max).then_inc(phi_ready, 1)

            def maxima(u, c, n):
                g = grp(u, c)
                wait(dve, mpc_ready, g)
                dve.wait_ge(sq_done, 8 * g + n + 1)
                v.tensor_reduce(nmax[:, n // 2, (n % 2) * HP:(n % 2 + 1) * HP],
                                s_q[n % 2][:, :].rearrange("p (h k) -> p h k", k=S),
                                axis=AX.X, op=ALU.max, negate=True).then_inc(max_ready, 1)

            def k_masked(u, c):
                g = grp(u, c)
                wait(dve, khi_ready, g)
                wait(dve, kres_ready, g)
                dve.wait_ge(k_done, g + 1)
                v.tensor_tensor(k_f[:, :], f_c[:, :], mk_sb[c % 2][:, :], ALU.mult).then_inc(kf_ready, 1)

            def reciprocals0(u, c, i):
                g = grp(u, c)
                n, d = 2 * (2 * g + 1 - i), den0[:, 2 * i:2 * i + 2]
                f, w = (f_c, f_x)[i], D + 1
                dve.wait_ge(av_done, 2 * g + 2 - i)
                wait(dve, y_ready, 4 * g)
                v.tensor_scalar(d, f[:, 0:2 * w].rearrange("p (n w) -> p n w", w=w)[:, :, D],
                                ATTN_EPS, None, ALU.add).then_inc(den0_step, 1)
                dve.wait_ge(den0_step, n + 1)
                v.reciprocal(d, d).then_inc(den0_step, 1)

            def attended0(u, c, i):
                g, p = grp(u, c), c % 2
                f, w = (f_c, f_x)[i], D + 1
                wait(dve, n_ready, g)
                dve.wait_ge(den0_step, 2 * (2 * g + 1 - i) + 2)
                for n in range(2):
                    j = 2 * i + n
                    v.scalar_tensor_tensor(out=y_sb[:, j, :], in0=f[:, n * w:n * w + D],
                                           scalar=den0[:, j:j + 1], in1=x_sb[p][:, j, :],
                                           op0=ALU.mult, op1=ALU.add).then_inc(y_ready, 1)

            def statistics(u, c, y_ready, per_group, y, st, stats_step):
                g = grp(u, c)
                dve.wait_ge(y_ready, per_group * (g + 1))
                wait(dve, stats_step, 2 * g)
                for j in range(PAIRS):
                    last = v.bn_stats(st[:, j, :], y[:, j, :])
                last.then_inc(stats_step, 1)

            def moments(u, c, st, mv, ve, stats_step, var_ready):
                g = grp(u, c)
                wait_alone(dve, stats_step, 2 * g + 1)
                for j in range(PAIRS):
                    last = v.bn_aggr(mv[:, j, :], st[:, j, :])
                last.then_inc(stats_step, 1)
                dve.wait_ge(stats_step, 2 * g + 2)
                v.tensor_scalar(ve[:, :], mv[:, :, 1], LN_EPS, None, ALU.add).then_inc(var_ready, 1)

            def offset(u, c, mv, rs, nb, rstd_ready, nb_ready):
                dve.wait_ge(rstd_ready, grp(u, c) + 1)
                v.scalar_tensor_tensor(out=nb[:, :], in0=mv[:, :, 0], scalar=-1.0, in1=rs[:, :],
                                       op0=ALU.mult, op1=ALU.mult).then_inc(nb_ready, 1)

            def q_residual(u, c):
                g, p = grp(u, c), c % 2
                dve.wait_ge(qhi_ready, g + 1)
                wait(dve, qlo_ready, g)
                v.tensor_tensor(r_q[:, :], f_v[:, :], q_pc[p][:, 0, :], ALU.subtract).then_inc(qres_ready, 1)

            def newton_product(u, c, j):
                n = 4 * grp(u, c) + j
                dve.wait_ge(r0_ready, n + 1)
                wait(dve, norm_step, 2 * n)
                v.tensor_tensor(flat(tden), o_bank[j % 2][:, 2 * P:4 * P], flat(rden[j % 2]), ALU.mult).then_inc(norm_step, 1)

            def newton_step(u, c, j):
                n = 4 * grp(u, c) + j
                dve.wait_ge(norm_step, 2 * n + 1)
                v.scalar_tensor_tensor(out=flat(rden[j % 2]), in0=flat(tden), scalar=2.0, in1=flat(rden[j % 2]),
                                       op0=ALU.subtract, op1=ALU.mult).then_inc(norm_step, 1)

            def normalise(u, c, j):
                g = grp(u, c)
                wait(dve, wo_done, g)
                dve.wait_ge(norm_step, 2 * (4 * g + j) + 2)
                v.tensor_tensor(flat(o_t[j]), o_bank[j % 2][:, 0:2 * P], flat(rden[j % 2]), ALU.mult).then_inc(o_ready, 1)

            def residual(u, c):
                g, p = grp(u, c), c % 2
                dve.wait_ge(res_ready, g + 1)
                wait(dve, z_ready, g)
                dve.wait_ge(wo_done, g + 1)
                v.tensor_tensor(y2[:, :, :].rearrange("p j d -> p (j d)"), w_ps[:, :],
                                res[p][:, :, :].rearrange("p j d -> p (j d)"), ALU.add).then_inc(y2_ready, 1)

            def slot(ahead, lag0, lag1, lag2, lag3):
                if lag2:
                    maxima(*lag2, 7)
                if lag3:
                    normalise(*lag3, 1)
                    newton_product(*lag3, 2)
                    newton_step(*lag3, 2)
                if lag0:
                    clip(*lag0, 0)
                if lag3:
                    normalise(*lag3, 2)
                if lag0:
                    clip(*lag0, 1)
                    features(*lag0, 0)
                    features(*lag0, 1)
                if lag3:
                    newton_product(*lag3, 3)
                    newton_step(*lag3, 3)
                    normalise(*lag3, 3)
                if lag1:
                    q_residual(*lag1)
                if lag0:
                    k_masked(*lag0)
                if lag3:
                    residual(*lag3)
                if lag0:
                    reciprocals0(*lag0, 1)
                if lag3:
                    statistics(*lag3, y2_ready, 1, y2, st1, stats1_step)
                if lag0:
                    reciprocals0(*lag0, 0)
                    attended0(*lag0, 1)
                    attended0(*lag0, 0)
                if lag3:
                    moments(*lag3, st1, mv1, ve1, stats1_step, var1_ready)
                if lag0:
                    statistics(*lag0, y_ready, 4, y_sb, st0, stats0_step)
                if lag2:
                    newton_product(*lag2, 0)
                if lag0:
                    moments(*lag0, st0, mv0, ve0, stats0_step, var0_ready)
                if lag2:
                    newton_step(*lag2, 0)
                if lag3:
                    offset(*lag3, mv1, rs1, nb1, rstd1_ready, nb1_ready)
                if lag2:
                    normalise(*lag2, 0)
                if lag1:
                    maxima(*lag1, 0)
                    maxima(*lag1, 1)
                if lag2:
                    newton_product(*lag2, 1)
                if lag1:
                    maxima(*lag1, 2)
                    maxima(*lag1, 3)
                if lag0:
                    offset(*lag0, mv0, rs0, nb0, rstd0_ready, nb0_ready)
                if lag1:
                    maxima(*lag1, 4)
                    maxima(*lag1, 5)
                if lag2:
                    newton_step(*lag2, 1)
                if lag1:
                    maxima(*lag1, 6)

            slots(dve, slot)

        @block.gpsimd
        def _(pool):
            gp = nc.gpsimd
            gp.memset(ident[:, :], 0.0).then_inc(pool_step, 1)
            pool.wait_ge(pool_step, 1)
            gp.affine_select(out=ident[:, :], in_=ident[:, :], compare_op=ALU.not_equal, fill=1.0,
                             base=0, pattern=[[-1, P]], channel_multiplier=1).then_inc(set_pool, 1)
            gp.memset(minus_half[:, :], -0.5)
            gp.memset(ones[:, :, :, :], 1.0)
            for p in range(2):
                last = gp.memset(k_st[p][:, :, :, :, :].rearrange("p h b a s -> p (h b a s)").bitcast(U32), 0)
            last.then_inc(k_zeroed, 1)
            pool.wait_ge(w_in, 16 * 11)
            gp.tensor_tensor(b0_row[:, :], b0_row[:, :], bo_row[:, :], ALU.add)
            gp.tensor_scalar(w_o[:, :, :], w_o[:, :, :], -1.0, None, ALU.mult)
            gp.tensor_scalar(w_q[:, :], w_q[:, :], float(HD) ** -0.5, None, ALU.mult).then_inc(w_scaled, 1)
            pool.wait_ge(w_scaled, 1)

            def k_residual(u, c):
                g, p = grp(u, c), c % 2
                wait(pool, klo_ready, g)
                pool.wait_ge(khi_ready, g + 1)
                gp.tensor_tensor(r_k[:, :], k_f[:, :], k_pc[p][:, 0, :], ALU.subtract).then_inc(kres_ready, 1)

            def k_low(u, c):
                g, p = grp(u, c), c % 2
                pool.wait_ge(kmid_ready, g + 1)
                wait(pool, k_stacked[p], 16 * 13 * uses(u, c - 2))
                gp.tensor_tensor(k_pc[p][:, 2, :], r_k[:, :], k_pc[p][:, 1, :], ALU.subtract).then_inc(klo_ready, 1)

            def rstd(u, c, var_ready, ve, rs, rstd_ready):
                pool.wait_ge(var_ready, grp(u, c) + 1)
                gp.tensor_tensor(rs[:, :], ve[:, :], minus_half[:, :], ALU.pow).then_inc(rstd_ready, 1)

            def rows(row):
                return row[:, :].rearrange("p (o d) -> p o d", o=1).to_broadcast([P, PAIRS, D])

            def residual_scale(u, c):
                g, p = grp(u, c), c % 2
                pool.wait_ge(n_ready, g + 1)
                wait(pool, y2_ready, g - 1)
                gp.tensor_tensor(res[p][:, :, :], n_sb[p][:, :, :], rows(g0_row), ALU.mult).then_inc(pool_step, 1)

            def residual(u, c):
                g, p = grp(u, c), c % 2
                pool.wait_ge(pool_step, g + 2)
                gp.tensor_tensor(res[p][:, :, :], res[p][:, :, :], rows(b0_row), ALU.add).then_inc(res_ready, 1)

            def max_pieces(u, c):
                g = grp(u, c)
                m = nmax[:, :, :].rearrange("p j (h a) -> p j a h", a=2)
                wait(pool, mT_done, g)
                pool.wait_ge(max_ready, 8 * (g + 1))
                gp.tensor_tensor(m_pc[:, :, :, 0, :], m, ones[:, :, :, :], ALU.mult).then_inc(piece_step, 1)
                pool.wait_ge(piece_step, 3 * g + 1)
                gp.tensor_tensor(r_m[:, :, :, :], m, m_pc[:, :, :, 0, :], ALU.subtract).then_inc(piece_step, 1)
                pool.wait_ge(piece_step, 3 * g + 2)
                gp.tensor_tensor(m_pc[:, :, :, 1, :], r_m[:, :, :, :], ones[:, :, :, :], ALU.mult).then_inc(piece_step, 1)
                pool.wait_ge(piece_step, 3 * g + 3)
                gp.tensor_tensor(m_pc[:, :, :, 2, :], r_m[:, :, :, :], m_pc[:, :, :, 1, :],
                                 ALU.subtract).then_inc(mpc_ready, 1)

            def q_low(u, c):
                g, p = grp(u, c), c % 2
                pool.wait_ge(qmid_ready, g + 1)
                wait(pool, q_stacked[p], 16 * 6 * uses(u, c - 2))
                gp.tensor_tensor(q_pc[p][:, 2, :], r_q[:, :], q_pc[p][:, 1, :], ALU.subtract).then_inc(qlo_ready, 1)

            def outputs_scale(u, c):
                g, p = grp(u, c), c % 2
                pool.wait_ge(z_ready, g + 1)
                wait(pool, out_saved[p], 16 * uses(u, c - 2))
                gp.tensor_tensor(o_sb[p][:, :, :], z_sb[:, :, :], rows(g1_row), ALU.mult).then_inc(pool_out_step, 1)

            def outputs(u, c):
                g, p = grp(u, c), c % 2
                pool.wait_ge(pool_out_step, g + 1)
                gp.tensor_tensor(o_sb[p][:, :, :], o_sb[p][:, :, :], rows(b1_row), ALU.add).then_inc(out_ready, 1)

            def slot(ahead, lag0, lag1, lag2, lag3):
                if lag0:
                    q_low(*lag0)
                if lag3:
                    outputs(*lag3)
                if lag2:
                    rstd(*lag2, var1_ready, ve1, rs1, rstd1_ready)
                if ahead:
                    k_residual(*ahead)
                    rstd(*ahead, var0_ready, ve0, rs0, rstd0_ready)
                if lag0:
                    residual_scale(*lag0)
                    max_pieces(*lag0)
                if ahead:
                    k_low(*ahead)
                if lag0:
                    residual(*lag0)
                if lag2:
                    outputs_scale(*lag2)

            slots(pool, slot)


def kernel(x, ctx_1024, mask_BxS2_ff1, L0_xattn_gamma, L0_xattn_beta, L1_xattn_wq, L1_xattn_wk, L1_xattn_wv,
           L1_xattn_wo, L1_xattn_bo, L1_xattn_ln_gamma, L1_xattn_ln_beta):
    import numpy as np
    import concourse.bacc as bacc
    from concourse.bass_utils import run_bass_kernel_spmd

    def by_row(w):
        return np.asarray(w).reshape(D, HP, 2 * HD).transpose(0, 2, 1).reshape(D, D)

    wo = np.asarray(L1_xattn_wo).reshape(2, HP // 2, 1, 2 * HD, D)
    wo2 = np.repeat(wo, 2, axis=2).transpose(1, 2, 3, 0, 4).reshape(P, 2, D)
    arrays = {"x": x, "ctx": ctx_1024, "mask": mask_BxS2_ff1, "g0": L0_xattn_gamma, "b0": L0_xattn_beta,
              "wq": by_row(L1_xattn_wq), "wk": by_row(L1_xattn_wk), "wv": L1_xattn_wv, "wo2": wo2,
              "bo": L1_xattn_bo, "g1": L1_xattn_ln_gamma, "b1": L1_xattn_ln_beta}
    wv = np.asarray(L1_xattn_wv).reshape(D, HP, 2, HD).transpose(0, 2, 1, 3).reshape(D, D)
    arrays["wv"] = wv
    arrays = {f"in_{k}": np.ascontiguousarray(a) for k, a in arrays.items()}
    nc = bacc.Bacc("TRN2", target_bir_lowering=False, num_devices=1)
    args = [nc.dram_tensor(k, a.shape, F32, kind="ExternalInput").ap() for k, a in arrays.items()]
    args.append(nc.dram_tensor("out_0", x.shape, F32, kind="ExternalOutput").ap())
    xattn_kernel(nc, *args)
    r = run_bass_kernel_spmd(nc, [arrays], core_ids=[0])
    return r.results[0]["out_0"]
```
